# Optimizing a Trainium2 kernel written in Bass

```python
import numpy as np
import jax
import jax.numpy as jnp

def _softmax(x, axis=-1):
    return jax.nn.softmax(x, axis=axis)

def _gelu(x):
    return jax.nn.gelu(x, approximate=True)

def _silu(x):
    return jax.nn.silu(x)

def _sigmoid(x):
    return jax.nn.sigmoid(x)

def _layernorm(x, axis=-1, eps=1e-05):
    m = jnp.mean(x, axis=axis, keepdims=True)
    v = jnp.var(x, axis=axis, keepdims=True)
    return (x - m) / jnp.sqrt(v + eps)

def _scatter_add(tgt, idx, src, axis=0):
    return tgt.at[idx].add(src)

def _segment_sum(src, seg, n):
    return jax.ops.segment_sum(src, seg, n)
kernel_name = 'mk_macaron_d1_jaxref_r4_edfe48'

def setup_inputs(seed: int=0):
    np.random.seed(seed)
    _w = jnp.asarray

    def _L0_attn_setup():
        import jax, jax.numpy as jnp
        import numpy as np
        B, T, D = (2, 512, 256)
        H = 16
        HD = D // H
        WINDOW = 128
        N_GLOBAL = 1
        SCALE = 1.0 / np.sqrt(HD)

        def _attend_mask(T):
            idx = jnp.arange(T)
            dist = jnp.abs(idx[:, None] - idx[None, :])
            attend = dist <= WINDOW
            glb = idx < N_GLOBAL
            attend = attend | glb[:, None] | glb[None, :]
            return attend
        key = jax.random.key(seed)
        ks = jax.random.split(key, 5)
        scale_w = 1.0 / np.sqrt(D)
        return {'x': jax.random.normal(ks[0], (B, T, D), dtype=jnp.float32), 'Wq': jax.random.normal(ks[1], (D, D), dtype=jnp.float32) * scale_w, 'Wk': jax.random.normal(ks[2], (D, D), dtype=jnp.float32) * scale_w, 'Wv': jax.random.normal(ks[3], (D, D), dtype=jnp.float32) * scale_w, 'Wo': jax.random.normal(ks[4], (D, D), dtype=jnp.float32) * scale_w}
    _L0_attn_in = _L0_attn_setup()

    def _L0_ffn_setup():
        import jax, jax.numpy as jnp
        import numpy as np
        CAPACITY_FACTOR = 1.25
        key = jax.random.key(seed)
        ks = jax.random.split(key, 6)
        B, S, H, E = (4, 1024, 256, 8)
        scale = 1.0 / np.sqrt(H)
        return {'tokens': jax.random.normal(ks[0], (B, S, H), dtype=jnp.float32), 'gate_w': jax.random.normal(ks[1], (E, H), dtype=jnp.float32) * scale, 'w1': jax.random.normal(ks[2], (E, H, H), dtype=jnp.float32) * scale, 'b1': jax.random.normal(ks[3], (E, H), dtype=jnp.float32) * 0.01, 'w2': jax.random.normal(ks[4], (E, H, H), dtype=jnp.float32) * scale, 'b2': jax.random.normal(ks[5], (E, H), dtype=jnp.float32) * 0.01}
    _L0_ffn_in = _L0_ffn_setup()
    _d = {'L0_attn_x': _L0_attn_in['x'], 'L0_attn_Wq': _L0_attn_in['Wq'], 'L0_attn_Wk': _L0_attn_in['Wk'], 'L0_attn_Wv': _L0_attn_in['Wv'], 'L0_attn_Wo': _L0_attn_in['Wo'], 'L0_ffn_gate_w': _L0_ffn_in['gate_w'], 'L0_ffn_w1': _L0_ffn_in['w1'], 'L0_ffn_b1': _L0_ffn_in['b1'], 'L0_ffn_w2': _L0_ffn_in['w2'], 'L0_ffn_b2': _L0_ffn_in['b2']}
    _x0 = _d['L0_attn_x']
    _d['L0_attn_x'] = jax.random.normal(jax.random.fold_in(jax.random.key(seed), 1), (4, 2048, 256), dtype=_x0.dtype)
    del _x0
    return _d

def reference(L0_attn_x, L0_attn_Wq, L0_attn_Wk, L0_attn_Wv, L0_attn_Wo, L0_ffn_gate_w, L0_ffn_w1, L0_ffn_b1, L0_ffn_w2, L0_ffn_b2):

    def _L0_attn_ref(x, Wq, Wk, Wv, Wo):
        import jax, jax.numpy as jnp
        import numpy as np
        B, T, D = (2, 512, 256)
        H = 16
        HD = D // H
        WINDOW = 128
        N_GLOBAL = 1
        SCALE = 1.0 / np.sqrt(HD)

        def _attend_mask(T):
            idx = jnp.arange(T)
            dist = jnp.abs(idx[:, None] - idx[None, :])
            attend = dist <= WINDOW
            glb = idx < N_GLOBAL
            attend = attend | glb[:, None] | glb[None, :]
            return attend
        Bb, Tt, Dd = x.shape
        q = (x @ Wq.T).reshape(Bb, Tt, H, HD).transpose(0, 2, 1, 3)
        k = (x @ Wk.T).reshape(Bb, Tt, H, HD).transpose(0, 2, 1, 3)
        v = (x @ Wv.T).reshape(Bb, Tt, H, HD).transpose(0, 2, 1, 3)
        attend = _attend_mask(Tt)
        logits = jnp.einsum('bhqd,bhkd->bhqk', q, k) * SCALE
        logits = jnp.where(attend[None, None, :, :], logits, -jnp.inf)
        weights = jax.nn.softmax(logits, axis=-1)
        weights = jnp.nan_to_num(weights)
        out = jnp.einsum('bhqk,bhkd->bhqd', weights, v)
        out = out.transpose(0, 2, 1, 3).reshape(Bb, Tt, Dd)
        return out @ Wo.T

    def _L0_ffn_ref(tokens, gate_w, w1, b1, w2, b2):
        import jax, jax.numpy as jnp
        import numpy as np
        CAPACITY_FACTOR = 1.25
        B, S, H = tokens.shape
        E = gate_w.shape[0]
        N = B * S
        cap = int(CAPACITY_FACTOR * N / E)
        x = tokens.reshape(N, H)
        probs = jax.nn.softmax(x @ gate_w.T, axis=-1)
        top2_w, top2_idx = jax.lax.top_k(probs, 2)
        a_e = top2_idx.reshape(-1)
        a_w = top2_w.reshape(-1)
        tok_id = jnp.arange(2 * N) // 2
        counts = jnp.bincount(a_e, length=E)
        keep = counts <= cap
        valid = keep[a_e]
        onehot = jax.nn.one_hot(a_e, E, dtype=jnp.int32)
        pos = jnp.take_along_axis(jnp.cumsum(onehot, axis=0) - 1, a_e[:, None], axis=1)[:, 0]
        p = jnp.where(valid, jnp.minimum(pos, cap - 1), cap)
        x_a = x[tok_id]
        buf = jnp.zeros((E, cap + 1, H), dtype=x.dtype).at[a_e, p].set(x_a)
        h = jax.nn.silu(jnp.einsum('ech,efh->ecf', buf, w1) + b1[:, None, :])
        y = jnp.einsum('ecf,egf->ecg', h, w2) + b2[:, None, :]
        contrib = y[a_e, p] * (a_w * valid.astype(x.dtype))[:, None]
        out = contrib.reshape(N, 2, H).sum(axis=1)
        return out.reshape(B, S, H)
    x = L0_attn_x
    x = x + 0.5 * _L0_ffn_ref(_layernorm(x, axis=-1), L0_ffn_gate_w, L0_ffn_w1, L0_ffn_b1, L0_ffn_w2, L0_ffn_b2)
    x = x + _L0_attn_ref(_layernorm(x, axis=-1), L0_attn_Wq, L0_attn_Wk, L0_attn_Wv, L0_attn_Wo)
    x = x + 0.5 * _L0_ffn_ref(_layernorm(x, axis=-1), L0_ffn_gate_w, L0_ffn_w1, L0_ffn_b1, L0_ffn_w2, L0_ffn_b2)
    return x

_drawn_inputs = setup_inputs


def setup_inputs(seed=0):
    import zlib

    import numpy as np

    out = dict(_drawn_inputs(seed))
    spreads = {}
    factors = {}
    for name, (base, spread) in spreads.items():
        noise = np.random.default_rng([zlib.crc32(name.encode()), seed]).standard_normal(out[name].shape)
        drawn = base * np.exp(spread * noise) if base else spread * noise
        out[name] = jnp.asarray(drawn.astype(out[name].dtype))
    for name, factor in factors.items():
        out[name] = (out[name] * factor).astype(out[name].dtype)
    return out
```

```python
import concourse.bass as bass
from concourse import mybir
from contextlib import ExitStack

FP32 = mybir.dt.float32
BF16 = mybir.dt.bfloat16
I32 = mybir.dt.int32
ALU = mybir.AluOpType
ACT = mybir.ActivationFunctionType
AX = mybir.AxisListType

B, T, D = 4, 2048, 256
H, HD = 16, 16
E = 8
N = B * T
CAPACITY = int(1.25 * N / E)
EPS = 1e-5
LOGIT_SCALE = 0.25
WINDOW = 128

P = 128
NT = T // P
KC = D // P
HG = 4
NG = H // HG
SP = 32
VW = HD + 1
WIN = 2 * WINDOW + SP
TERMS = 6
SLOTS = TERMS + 1
SLOT_PIECE2, SLOT_PIECE3 = 2, 5
KROWS = HD * TERMS
HALF = T // 2
MASKED = -1.0e30

C_IDENT = 0
C_BAND = C_IDENT + P
C_PICK = C_BAND + 3 * WIN
C_DIAG = C_PICK + NG * SP
C_RANK = C_DIAG + H * VW
C_END = C_RANK + E


def build(nc, x, wqk, wback, wv, wo, gate, w1, b1, w2, b2, consts, x1, out):
    ctx = ExitStack()
    with ctx:
        def sb(name, shape, dt=FP32):
            return ctx.enter_context(nc.sbuf_tensor(name, shape, dt))

        q_stack = [sb(f"q_stack{i}", [P, HG, T], BF16) for i in range(2)]
        k_stack = [sb(f"k_stack{i}", [P, HG, T + 2 * WINDOW], BF16) for i in range(2)]
        xnT = sb("xnT", [P, KC, T])
        v_sb = sb("v_sb", [P, NT, H * VW + SP - VW])
        probs = sb("probs", [P, 4, HG, 3 * P])
        attn = sb("attn", [P, NT, D])
        x_b = sb("x_b", [P, NT, D])
        piece0 = sb("piece0", [P, SLOTS, HALF], BF16)
        rest = sb("rest", [P, 2, 512])
        wqk_sb = sb("wqk_sb", [P, NG, KC, P])
        wback_sb = sb("wback_sb", [P, NG, D])
        wv_sb = sb("wv_sb", [P, KC, D])
        wo_sb = sb("wo_sb", [P, KC, D])
        gate_sb = sb("gate_sb", [P, KC, SP])
        con = sb("con", [P, C_END])
        ones = sb("ones", [P, P])
        neg_half = sb("neg_half", [P, 4])
        v0_all = sb("v0_all", [P, H * VW])
        o_raw = sb("o_raw", [P, 4 * P])
        o_add = sb("o_add", [P, 4, HG, VW])
        glob_term = sb("glob_term", [P, 4, HG, VW])
        recip = sb("recip", [P, 4, HG])
        s0T = sb("s0T", [P, NT, H])
        row_max = sb("row_max", [P, NG, HG, NT])
        p0_arg = sb("p0_arg", [P, NT, HG])
        p0 = sb("p0", [P, NG, NT, HG])
        neg_max = [sb(f"neg_max{i}", [NT * HG, P], BF16) for i in range(3)]
        neg_rest = sb("neg_rest", [NT * HG, P])
        logits = sb("logits", [P, B * NT, E])
        stats = sb("stats", [P, 4, 6])
        mean_var = sb("mean_var", [P, NT, 2])
        var_eps = sb("var_eps", [P, NT])
        rstd = sb("rstd", [P, NT])
        small = sb("small", [P, 64])
        flags = sb("flags", [1, E + 1], I32)

        probs_flat = probs[:, :, :, :].rearrange("p a h n -> p (a h n)")
        attn_flat = attn[:, :, :].rearrange("p t d -> p (t d)")
        piece = [piece0[:, :, :], x_b[:, :, :].rearrange("p t d -> p (t d)").bitcast(BF16)
                 [:, 0:SLOTS * HALF].rearrange("p (s n) -> p s n", s=SLOTS)]
        o0_norm = x_b[0:1, NT - 1, :].rearrange("p (h c) -> p h c", c=HD)
        xn = probs_flat[:, 0:8 * D].rearrange("p (t d) -> p t d", t=8)
        attnT = probs_flat[:, 2048:3072].rearrange("p (s k n) -> p s k n", s=2, k=KC)
        strip_rows = probs_flat[:, 3072:3584]
        sg_arg = probs_flat[:, 3584:3840].rearrange("p (m h) -> p m h", h=H)
        masked_o0 = probs_flat[:, 3840:3840 + H * VW]
        o0_row = probs_flat[0:1, 4112:4112 + H * VW]
        pgT = probs_flat[:, 4400:4400 + NT * SP].rearrange("p (m c) -> p m c", c=SP)
        uw = probs_flat[:, 4912:4912 + KC * SP].rearrange("p (k c) -> p k c", k=KC)
        first_scaled = probs_flat[:, 4976:4976 + NG * SP].rearrange("p (g c) -> p g c", g=NG)
        wts = rest[:, 0, :].rearrange("p (t e) -> p t e", e=E)
        ident = con[:, C_IDENT:C_IDENT + P]
        band = [con[:, C_BAND + i * WIN:C_BAND + (i + 1) * WIN] for i in range(3)]
        pick = con[:, C_PICK:C_PICK + NG * SP].rearrange("p (g c) -> p g c", g=NG)
        diag = con[:, C_DIAG:C_DIAG + H * VW]
        rank = con[:, C_RANK:C_RANK + E]
        v_heads = v_sb[:, :, 0:H * VW].rearrange("p t (h c) -> p t h c", c=VW)

        bank = [ctx.enter_context(nc.psum_tensor(f"bank{i}", [P, 512], FP32)) for i in range(2)]
        s_banks = ctx.enter_context(nc.psum_tensor("s_banks", [P, 4, 512], FP32))
        o_bank = ctx.enter_context(nc.psum_tensor("o_bank", [P, 512], FP32))
        misc = ctx.enter_context(nc.psum_tensor("misc", [P, 512], FP32))
        a_ring = [bank[0], bank[1], s_banks[:, 3, :]]
        S_RING = 3

        names = ["x_in0", "x_in1", "x_in2", "x_in3", "consts_in", "filled", "stats_ready", "moments_ready",
                 "eps_added", "rstd_ready", "xn_ready", "xnT_psum", "xnT_ready", "v_psum", "v_ready",
                 "gate_psum", "gate_rows", "gate_cols", "logits_ready",
                 "proj_in_psum", "proj_in_sbuf", "proj_psum", "x2_ready", "stored",
                 "pe_step", "dve_step", "act_step", "pool_step",
                 "misc_full", "misc_free", "piece1_ready", "piece2_ready", "piece3_ready", "slots_ready",
                 "stack00", "stack01", "stack10", "stack11", "a_full", "a_free",
                 "max_piece", "max_stacked", "p0_diff", "p0_arg_ready", "p0_ready",
                 "b_full", "exp_ready", "band_ready", "pv_done", "o_copied", "glob_ready", "o_added",
                 "attn_ready"]
        sems = {n: ctx.enter_context(nc.semaphore(n)) for n in names}
        nums = [s.num for s in sems.values()]
        assert max(nums) - min(nums) + 1 == len(nums)
        S = sems

        def reset():
            nc.all_engine_barrier(sems_to_clear=range(min(nums), max(nums) + 1))

        with nc.Block() as block:
            @block.sync
            def _(sp):
                for dst, src in ((con[:, :], consts), (wqk_sb[:, :, :, :], wqk), (wback_sb[:, :, :], wback),
                                 (wv_sb[:, :, :], wv), (wo_sb[:, :, :], wo), (gate_sb[:, :, 0:E], gate)):
                    sp.dma_start(dst, src).then_inc(S["consts_in"], 16)
                sp.wait_ge(S["consts_in"], 6 * 16)

            @block.vector
            def _(dve):
                dve.memset(ones[:, :], 1.0)
                dve.memset(neg_half[:, :], -0.5)
                dve.memset(gate_sb[:, :, E:SP], 0.0)
        reset()

        def norm_block(ntiles, load=None, gate_to=None, values=False, project=False, store=None):
            chunks = ntiles // 4
            pairs = ntiles // 2
            with nc.Block() as block:
                @block.sync
                def _(sp):
                    if load:
                        load(sp)
                    if store:
                        for c in range(chunks):
                            sp.wait_ge(S["x2_ready"], 2 * c + 2)
                            sp.dma_start(store(c), x_b[:, 4 * c:4 * c + 4, :]).then_inc(S["stored"], 16)
                        sp.wait_ge(S["stored"], 16 * chunks)

                @block.vector
                def _(dve):
                    def normalise(c):
                        dve.wait_ge(S["rstd_ready"], c + 1)
                        if c >= 2:
                            dve.wait_ge(S["xnT_psum"], 2 * c - 2)
                        for t in range(4 * c, 4 * c + 4):
                            dve.tensor_scalar(xn[:, t % 8, :], x_b[:, t, :], mean_var[:, t, 0:1],
                                              rstd[:, t:t + 1], ALU.subtract, ALU.mult)\
                               .then_inc(S["xn_ready"], 1)

                    def take_values(u):
                        dve.wait_ge(S["v_psum"], u + 1)
                        dve.tensor_copy(v_heads[:, 2 * u, :, 0:HD],
                                        s_banks[:, u % 2, 0:D].rearrange("p (h c) -> p h c", c=HD))
                        dve.tensor_copy(v_heads[:, 2 * u + 1, :, 0:HD],
                                        s_banks[:, u % 2, D:2 * D].rearrange("p (h c) -> p h c", c=HD))\
                           .then_inc(S["v_ready"], 1)

                    for c in range(chunks):
                        if project:
                            dve.wait_ge(S[f"x_in{c}"], 16)
                            for u in (2 * c, 2 * c + 1):
                                dve.wait_ge(S["proj_psum"], u + 1)
                                dve.tensor_tensor(
                                    x_b[:, 2 * u:2 * u + 2, :],
                                    s_banks[:, 2 + u % 2, :].rearrange("p (t d) -> p t d", t=2),
                                    x_b[:, 2 * u:2 * u + 2, :], ALU.add).then_inc(S["x2_ready"], 1)
                            dve.wait_ge(S["x2_ready"], 2 * c + 2)
                        else:
                            dve.wait_ge(S[f"x_in{c}"], 16)
                        if c:
                            dve.wait_ge(S["moments_ready"], 4 * c)
                        for t in range(4 * c, 4 * c + 4):
                            dve.bn_stats(stats[:, t % 4, :], x_b[:, t, :]).then_inc(S["stats_ready"], 1)
                        for t in range(4 * c, 4 * c + 4):
                            dve.wait_ge(S["stats_ready"], t + 1)
                            dve.bn_aggr(mean_var[:, t, :], stats[:, t % 4, :]).then_inc(S["moments_ready"], 1)
                        if c >= 1:
                            normalise(c - 1)
                            if values:
                                if c >= 2:
                                    take_values(2 * c - 4)
                                    take_values(2 * c - 3)
                    normalise(chunks - 1)
                    if values:
                        for u in range(max(2 * chunks - 4, 0), pairs):
                            take_values(u)
                    if gate_to is not None:
                        dve.wait_ge(S["gate_cols"], 1)
                        if ntiles == NT:
                            dve.tensor_copy(
                                gate_to().rearrange("p (g c) e -> p g c e", g=4),
                                s_banks[:, 3, :].rearrange("p (c g e) -> p g c e", c=4, g=4)[:, :, :, 0:E])\
                               .then_inc(S["logits_ready"], 1)

                @block.gpsimd
                def _(pool):
                    for c in range(chunks):
                        pool.wait_ge(S["moments_ready"], 4 * c + 4)
                        pool.tensor_scalar(var_eps[:, 4 * c:4 * c + 4], mean_var[:, 4 * c:4 * c + 4, 1],
                                           EPS, None, ALU.add).then_inc(S["eps_added"], 1)
                        pool.wait_ge(S["eps_added"], c + 1)
                        pool.tensor_tensor(rstd[:, 4 * c:4 * c + 4], var_eps[:, 4 * c:4 * c + 4],
                                           neg_half[:, :], ALU.pow).then_inc(S["rstd_ready"], 1)

                @block.scalar
                def _(act):
                    def take_attnT(u):
                        act.wait_ge(S["proj_in_psum"], u + 1)
                        if u >= 2:
                            act.wait_ge(S["proj_psum"], u - 1)
                        act.activation(attnT[:, u % 2, :, :],
                                       s_banks[:, u % 2, :].rearrange("p (k n) -> p k n", k=KC),
                                       ACT.Copy).then_inc(S["proj_in_sbuf"], 1)

                    def take_xnT(u):
                        act.wait_ge(S["xnT_psum"], u + 1)
                        act.activation(xnT[:, :, 2 * P * u:2 * P * (u + 1)],
                                       bank[u % 2][:, :].rearrange("p (k n) -> p k n", k=KC),
                                       ACT.Copy).then_inc(S["xnT_ready"], 1)

                    for c in range(chunks + 2):
                        if project and c < chunks:
                            take_attnT(2 * c)
                            take_attnT(2 * c + 1)
                        if c >= 2:
                            take_xnT(2 * c - 4)
                            take_xnT(2 * c - 3)
                    if gate_to is not None:
                        act.wait_ge(S["gate_psum"], 1)
                        act.activation(strip_rows, misc[:, :], ACT.Copy).then_inc(S["gate_rows"], 1)

                @block.tensor
                def _(pe):
                    def project_pair(u):
                        if u >= 2:
                            pe.wait_ge(S["proj_in_sbuf"], u - 1)
                        for k in range(KC):
                            for i in range(2):
                                last = pe.transpose(s_banks[:, u % 2, k * 2 * P + i * P:k * 2 * P + (i + 1) * P],
                                                    attn[:, 2 * u + i, k * P:(k + 1) * P], ident)
                        last.then_inc(S["proj_in_psum"], 1)

                    def project_out(u):
                        pe.wait_ge(S["proj_in_sbuf"], u + 1)
                        if u >= 2:
                            pe.wait_ge(S["x2_ready"], u - 1)
                        for i in range(2):
                            for k in range(KC):
                                last = pe.matmul(s_banks[:, 2 + u % 2, i * D:(i + 1) * D],
                                                 attnT[:, u % 2, k, i * P:(i + 1) * P], wo_sb[:, k, :],
                                                 start=(k == 0), stop=(k == KC - 1))
                        last.then_inc(S["proj_psum"], 1)

                    def transpose_pair(u):
                        pe.wait_ge(S["xn_ready"], 2 * u + 2)
                        if u >= 2:
                            pe.wait_ge(S["xnT_ready"], u - 1)
                        for k in range(KC):
                            for i in range(2):
                                last = pe.transpose(bank[u % 2][:, k * 2 * P + i * P:k * 2 * P + (i + 1) * P],
                                                    xn[:, (2 * u + i) % 8, k * P:(k + 1) * P], ident)
                        last.then_inc(S["xnT_psum"], 1)

                    def values_pair(u):
                        pe.wait_ge(S["xnT_ready"], u + 1)
                        if u >= 2:
                            pe.wait_ge(S["v_ready"], u - 1)
                        for i in range(2):
                            for k in range(KC):
                                last = pe.matmul(s_banks[:, u % 2, i * D:(i + 1) * D],
                                                 xnT[:, k, (2 * u + i) * P:(2 * u + i + 1) * P], wv_sb[:, k, :],
                                                 start=(k == 0), stop=(k == KC - 1))
                        last.then_inc(S["v_psum"], 1)

                    for c in range(chunks + 2):
                        if project and c < chunks:
                            for u in (2 * c, 2 * c + 1):
                                project_pair(u)
                                if u >= 1:
                                    project_out(u - 1)
                            project_out(2 * c + 1) if c == chunks - 1 else None
                        if c >= 2:
                            transpose_pair(2 * c - 4)
                            transpose_pair(2 * c - 3)
                            if values:
                                values_pair(2 * c - 4)
                                values_pair(2 * c - 3)
                    if gate_to is not None:
                        pe.wait_ge(S["xnT_ready"], pairs)
                        for k in range(KC):
                            for g in range(4):
                                last = pe.matmul(misc[SP * g:SP * (g + 1), :], gate_sb[:, k, :],
                                                 xnT[:, k, 512 * g:512 * (g + 1)],
                                                 start=(k == 0), stop=(k == KC - 1))
                        last.then_inc(S["gate_psum"], 1)
                        pe.wait_ge(S["gate_rows"], 1)
                        if project:
                            pe.wait_ge(S["x2_ready"], pairs)
                        for c in range(4):
                            last = pe.transpose(s_banks[:, 3, P * c:P * (c + 1)],
                                                strip_rows[:, P * c:P * (c + 1)], ident)
                        last.then_inc(S["gate_cols"], 1)
            reset()

        def load_batch(dram, b):
            def load(sp):
                for c in range(NT // 4):
                    sp.dma_start(x_b[:, 4 * c:4 * c + 4, :],
                                 dram[bass.ds(b, 1), 512 * c:512 * (c + 1), :]
                                 .rearrange("o (t p) d -> p (o t) d", p=P)).then_inc(S[f"x_in{c}"], 16)
            return load

        def route():
            L = B * NT
            tmp = [attn_flat[:, i * 512:(i + 1) * 512].rearrange("p (t e) -> p t e", e=E) for i in range(6)]
            row = [attn_flat[:, 3072 + i * L:3072 + (i + 1) * L] for i in range(4)]
            counts = attn_flat[:, 3600:3600 + E]
            keep = attn_flat[:, 3616:3616 + E + 1]

            def wide(r):
                return r.unsqueeze(2).to_broadcast([P, L, E])

            rank_all = rank.unsqueeze(1).to_broadcast([P, L, E])
            with nc.Block() as block:
                @block.vector
                def _(dve):
                    done = [0]

                    def step(ins):
                        done[0] += 1
                        ins.then_inc(S["dve_step"], 1)
                        dve.wait_ge(S["dve_step"], done[0])

                    step(dve.tensor_reduce(row[0], logits[:, :, :], AX.X, ALU.max))
                    step(dve.tensor_tensor(tmp[0], logits[:, :, :], wide(row[0]), ALU.subtract))
                    dve.wait_ge(S["act_step"], 1)
                    step(dve.tensor_reduce(row[1], tmp[1], AX.X, ALU.add))
                    step(dve.reciprocal(row[2], row[1]))
                    probs_e = tmp[0]
                    step(dve.tensor_tensor(probs_e, tmp[1], wide(row[2]), ALU.mult))

                    def pick_first_largest(values, selected, a):
                        step(dve.tensor_reduce(row[0], values, AX.X, ALU.max))
                        step(dve.tensor_tensor(a, values, wide(row[0]), ALU.is_equal))
                        step(dve.tensor_tensor(a, a, rank_all, ALU.mult))
                        step(dve.tensor_reduce(row[1], a, AX.X, ALU.max))
                        step(dve.tensor_tensor(selected, rank_all, wide(row[1]), ALU.is_equal))

                    pick_first_largest(probs_e, tmp[2], tmp[1])
                    step(dve.scalar_tensor_tensor(out=tmp[3], in0=tmp[2], scalar=-4.0, in1=probs_e,
                                                  op0=ALU.mult, op1=ALU.add))
                    pick_first_largest(tmp[3], tmp[4], tmp[1])
                    step(dve.tensor_tensor(tmp[2], tmp[2], tmp[4], ALU.add))
                    step(dve.tensor_reduce(counts, tmp[2].rearrange("p t e -> p e t"), AX.X, ALU.add))
                    dve.wait_ge(S["pe_step"], 1)
                    step(dve.tensor_scalar(keep[:, 0:E], misc[:, 0:E], float(CAPACITY), None, ALU.is_le))
                    step(dve.tensor_reduce(keep[:, E:E + 1], keep[:, 0:E], AX.X, ALU.max))
                    step(dve.tensor_copy(flags[0:1, :], keep[0:1, :]))
                    step(dve.tensor_tensor(tmp[3], tmp[2], probs_e, ALU.mult))
                    step(dve.scalar_tensor_tensor(out=wts[:, :, :], in0=tmp[3], scalar=0.5,
                                                  in1=keep[:, 0:E].unsqueeze(1).to_broadcast([P, L, E]),
                                                  op0=ALU.mult, op1=ALU.mult))

                @block.scalar
                def _(act):
                    act.wait_ge(S["dve_step"], 2)
                    act.activation(tmp[1], tmp[0], ACT.Exp).then_inc(S["act_step"], 1)

                @block.tensor
                def _(pe):
                    pe.wait_ge(S["dve_step"], 18)
                    pe.matmul(misc[:, 0:E], ones[:, :], counts, start=True, stop=True)\
                      .then_inc(S["pe_step"], 1)
            reset()
            return nc.values_load(flags[0:1, E:E + 1], min_val=0, max_val=1)

        def experts(src, dst):
            pool_w = v_sb[:, :, :].rearrange("p t c -> p (t c)")
            w1_sb = pool_w[:, 0:KC * D].rearrange("p (k n) -> p k n", k=KC)
            w2_sb = pool_w[:, 512:512 + KC * D].rearrange("p (k n) -> p k n", k=KC)
            b1_sb = pool_w[:, 1024:1024 + KC]
            b2_sb = pool_w[0:1, 1280:1280 + D]
            hT = pool_w[:, 1536:1536 + KC * 512].rearrange("p (k n) -> p k n", k=KC)
            weight = pool_w[:, 2600:2604]

            def chunk_of(dram, c):
                return dram.rearrange("b t d -> (b t) d").rearrange("(c t p) d -> c p t d", t=4, p=P)[
                    bass.ds(c, 1)].rearrange("o p t d -> p (o t) d")

            with nc.Fori(0, N // 512) as c:
                norm_block(4, load=lambda sp: sp.dma_start(x_b[:, 0:4, :], chunk_of(src, c))
                           .then_inc(S["x_in0"], 16))
                with nc.Fori(0, E) as e:
                    kept = nc.values_load(flags[0:1, bass.ds(e, 1)], min_val=0, max_val=1)
                    with nc.If(kept != 0):
                        with nc.Block() as block:
                            @block.sync
                            def _(sp):
                                for to, frm in ((w1_sb, w1[bass.ds(e, 1)].rearrange("o p k n -> p (o k) n")),
                                                (w2_sb, w2[bass.ds(e, 1)].rearrange("o p k n -> p (o k) n")),
                                                (b1_sb, b1[bass.ds(e, 1)].rearrange("o p k -> p (o k)")),
                                                (b2_sb, b2[bass.ds(e, 1), :])):
                                    sp.dma_start(to, frm).then_inc(S["consts_in"], 16)

                            @block.tensor
                            def _(pe):
                                pe.wait_ge(S["consts_in"], 64)
                                for f in range(KC):
                                    for k in range(KC):
                                        last = pe.matmul(bank[f][:, :], w1_sb[:, k, f * P:(f + 1) * P],
                                                         xnT[:, k, 0:512], start=(k == 0), stop=(k == KC - 1))
                                    last.then_inc(S["pe_step"], 1)
                                pe.wait_ge(S["act_step"], 2 * KC)
                                for t in range(4):
                                    o = s_banks[:, t, 0:D]
                                    for k in range(KC):
                                        pe.matmul(o, hT[:, k, t * P:(t + 1) * P], w2_sb[:, k, :],
                                                  start=(k == 0), stop=False)
                                    pe.matmul(o, ones[0:1, :], b2_sb, start=False, stop=True)\
                                      .then_inc(S["pe_step"], 1)

                            @block.scalar
                            def _(act):
                                act.wait_ge(S["consts_in"], 64)
                                for f in range(KC):
                                    act.wait_ge(S["pe_step"], f + 1)
                                    act.activation(hT[:, f, :], bank[f][:, :], ACT.Silu,
                                                   bias=b1_sb[:, f:f + 1]).then_inc(S["act_step"], 2)

                            @block.gpsimd
                            def _(pool):
                                pool.tensor_copy(weight, wts[:, bass.ds(c * 4, 4), bass.ds(e, 1)]
                                                 .rearrange("p t o -> p (t o)")).then_inc(S["pool_step"], 1)

                            @block.vector
                            def _(dve):
                                dve.wait_ge(S["pool_step"], 1)
                                for t in range(4):
                                    dve.wait_ge(S["pe_step"], KC + t + 1)
                                    dve.scalar_tensor_tensor(out=x_b[:, t, :], in0=s_banks[:, t, 0:D],
                                                             scalar=weight[:, t:t + 1], in1=x_b[:, t, :],
                                                             op0=ALU.mult, op1=ALU.add)
                        reset()
                with nc.Block() as block:
                    @block.sync
                    def _(sp):
                        sp.dma_start(chunk_of(dst, c), x_b[:, 0:4, :]).then_inc(S["stored"], 16)
                        sp.wait_ge(S["stored"], 16)
                reset()

        def first_token_block():
            with nc.Block() as block:
                @block.tensor
                def _(pe):
                    for g in range(NG):
                        for k in range(KC):
                            last = pe.matmul(bank[0][:, g:g + 1], wqk_sb[:, g, k, :], xnT[:, k, 0:1],
                                             start=(k == 0), stop=(k == KC - 1))
                    last.then_inc(S["pe_step"], 1)
                    pe.wait_ge(S["filled"], 1)
                    pe.matmul(o_bank[:, 0:H * VW], ones[0:1, :], v_sb[0:1, 0, 0:H * VW],
                              start=True, stop=True).then_inc(S["pe_step"], 1)
                    pe.wait_ge(S["dve_step"], NG)
                    for k in range(KC):
                        for g in range(NG):
                            last = pe.matmul(bank[1][:, k * SP:(k + 1) * SP], wback_sb[:, g, k * P:(k + 1) * P],
                                             first_scaled[:, g, :], start=(g == 0), stop=(g == NG - 1))
                    last.then_inc(S["pe_step"], 1)
                    pe.wait_ge(S["dve_step"], NG + 1)
                    for k in range(KC):
                        for g in range(4):
                            last = pe.matmul(misc[SP * g:SP * (g + 1), :], uw[:, k, :],
                                             xnT[:, k, 512 * g:512 * (g + 1)],
                                             start=(k == 0), stop=(k == KC - 1))
                    last.then_inc(S["pe_step"], 1)
                    pe.wait_ge(S["act_step"], 1)
                    for c in range(4):
                        last = pe.transpose(s_banks[:, 0, P * c:P * (c + 1)],
                                            strip_rows[:, P * c:P * (c + 1)], ident)
                    last.then_inc(S["pe_step"], 1)
                    pe.wait_ge(S["dve_step"], NG + 2)
                    pe.transpose(bank[0][0:1, 128:256], small[:, 0:1], ident).then_inc(S["pe_step"], 1)
                    pe.wait_ge(S["dve_step"], NG + 4)
                    pe.matmul(bank[1][:, 256:256 + H], ones[0:1, :], small[0:1, 32:32 + H],
                              start=True, stop=True).then_inc(S["pe_step"], 1)
                    pe.wait_ge(S["act_step"], 2)
                    pe.wait_ge(S["pool_step"], 1)
                    for m in range(NT):
                        s = m // 4
                        tile = 4 * (m % 4) + m // 4
                        last = pe.matmul(s_banks[SP * s:SP * (s + 1), 1, 0:H * VW], pgT[:, m, :],
                                         v_sb[:, tile, 0:H * VW], start=(m % 4 == 0), stop=(m % 4 == 3))
                    last.then_inc(S["pe_step"], 1)
                    pe.wait_ge(S["dve_step"], NG + 7)
                    pe.matmul(s_banks[0:1, 2, 0:H * VW], ones[:, 0:1], masked_o0,
                              start=True, stop=True).then_inc(S["pe_step"], 1)

                @block.scalar
                def _(act):
                    act.wait_ge(S["pe_step"], 4)
                    act.activation(strip_rows, misc[:, :], ACT.Copy).then_inc(S["act_step"], 1)
                    act.wait_ge(S["dve_step"], NG + 6)
                    act.activation(pgT[:, :, 0:H], sg_arg, ACT.Exp, scale=LOGIT_SCALE)\
                       .then_inc(S["act_step"], 1)

                @block.gpsimd
                def _(pool):
                    pool.memset(v_heads[:, :, :, HD], 1.0).then_inc(S["filled"], 1)
                    pool.memset(v_sb[:, :, H * VW:], 0.0)
                    pool.memset(pgT[:, :, H:SP], 0.0).then_inc(S["pool_step"], 1)

                @block.vector
                def _(dve):
                    dve.wait_ge(S["pe_step"], 1)
                    for g in range(NG):
                        dve.tensor_scalar(first_scaled[:, g, :], pick[:, g, :], bank[0][:, g:g + 1], None,
                                          ALU.mult).then_inc(S["dve_step"], 1)
                    dve.wait_ge(S["pe_step"], 3)
                    dve.tensor_copy(uw[:, :, :], bank[1][:, 0:KC * SP].rearrange("p (k c) -> p k c", k=KC))\
                       .then_inc(S["dve_step"], 1)
                    dve.wait_ge(S["act_step"], 1)
                    dve.tensor_reduce(small[:, 0:1], strip_rows, AX.X, ALU.max)\
                       .then_inc(S["dve_step"], 1)
                    dve.wait_ge(S["pe_step"], 5)
                    cols = s_banks[:, 0, :].rearrange("p (c g e) -> p c g e", c=4, g=4)
                    dve.tensor_copy(s0T[:, :, :].rearrange("p (g c) h -> p g c h", g=4),
                                    cols.rearrange("p c g e -> p g c e")[:, :, :, H:2 * H])\
                       .then_inc(S["dve_step"], 1)
                    dve.wait_ge(S["pe_step"], 6)
                    dve.tensor_reduce(small[0:1, 32:32 + SP],
                                      bank[0][0:1, 128:256].rearrange("p (g e) -> p e g", g=4),
                                      AX.X, ALU.max).then_inc(S["dve_step"], 1)
                    dve.wait_ge(S["pe_step"], 7)
                    dve.tensor_copy(small[:, 8:8 + H], bank[1][:, 256:256 + H])\
                       .then_inc(S["dve_step"], 1)
                    dve.wait_ge(S["dve_step"], NG + 5)
                    dve.tensor_tensor(sg_arg,
                                      s_banks[:, 0, :].rearrange("p (m e) -> p m e", m=NT)[:, :, 0:H],
                                      small[:, 8:8 + H].unsqueeze(1).to_broadcast([P, NT, H]),
                                      ALU.subtract).then_inc(S["dve_step"], 1)
                    dve.tensor_copy(v0_all[:, :], o_bank[:, 0:H * VW])
                    dve.wait_ge(S["pe_step"], 8)
                    dve.tensor_tensor(masked_o0, s_banks[:, 1, 0:H * VW], diag, ALU.mult)\
                       .then_inc(S["dve_step"], 1)
                    dve.wait_ge(S["pe_step"], 9)
                    dve.tensor_copy(o0_row, s_banks[0:1, 2, 0:H * VW])\
                       .then_inc(S["dve_step"], 1)
                    dve.wait_ge(S["dve_step"], NG + 8)
                    heads = o0_row.rearrange("p (h c) -> p h c", c=VW)
                    dve.reciprocal(small[0:1, 48:48 + H], heads[:, :, HD]).then_inc(S["dve_step"], 1)
                    dve.wait_ge(S["dve_step"], NG + 9)
                    dve.tensor_tensor(o0_norm, heads[:, :, 0:HD],
                                      small[0:1, 48:48 + H].unsqueeze(2).to_broadcast([1, H, HD]), ALU.mult)
            reset()

        A_STEPS = NG * NT
        LAG_B, LAG_PV, LAG_OUT = NT + 3, NT + 6, NT + 7
        STEPS = A_STEPS + LAG_OUT + 1
        QK_AT = {3: 0, 7: 1, 11: 2, 15: 3}
        SLOTS_AT = {9: (0, (0, 1)), 10: (0, (2, 3)), 17: (1, (0, 1)), 18: (1, (2, 3))}

        def band_count(n):
            g, j = divmod(n, NT)
            return g * (2 * NT - 2) + min(1 + 2 * j, 2 * NT - 2)

        def next_groups(k, at):
            return [g for g in range(1, NG) if k - NT * (g - 1) == at]

        def events(k):
            a, b = k < A_STEPS, 0 <= k - LAG_B < A_STEPS
            turn = 0 <= k - LAG_OUT < A_STEPS and (k - LAG_OUT) % 4 == 3
            quartet = (k - LAG_OUT) // 4
            for half, at in enumerate((12, 19)):
                for g in next_groups(k, at):
                    yield "STACK", (g, half)
            for h in range(HG):
                if a:
                    yield "A", (k, h)
                if h == 0:
                    if 0 <= k - LAG_PV < A_STEPS:
                        yield "PV", k - LAG_PV
                    if turn:
                        yield "TURN", quartet
                    for at, c in QK_AT.items():
                        for g in next_groups(k, at + 1):
                            yield "PIECE1", (g, c)
                    if k > NT and k % NT == 1 and k <= A_STEPS + 1:
                        yield "MAX", k // NT - 1
                if b:
                    yield "B", (k - LAG_B, h)
                if h == 1 and 0 <= k - LAG_PV < A_STEPS and (k - LAG_PV) % 4 == 3:
                    yield "COPY_OUT", (k - LAG_PV) // 4
                if h == 1 and turn:
                    yield "OUT", quartet
                if h >= 2:
                    for at, c in QK_AT.items():
                        for g in next_groups(k, at):
                            yield "QK", (g, c, h - 2)
            if b:
                yield "CUT", k - LAG_B
            if 0 <= k + 1 - LAG_OUT < A_STEPS and (k + 1 - LAG_OUT) % 4 == 3:
                yield "GLOB", (k + 1 - LAG_OUT) // 4
            for at, c in QK_AT.items():
                for g in next_groups(k, at + 1):
                    yield "SPLIT", (g, c)
            for at, (half, copies) in SLOTS_AT.items():
                for g in next_groups(k, at):
                    yield "SLOTS", (g, half, copies)

        def window(j):
            return (P if j == 0 else 0), (2 * P if j == NT - 1 else 3 * P)

        STACK_DMAS = 2 * HG

        MAX_STACKED = 16 * 3

        def stack_sem(g, half):
            return S[f"stack{g % 2}{half}"]

        def stacked(g):
            return 16 * STACK_DMAS * (g // 2 + 1)

        def band_block():
            with nc.Block() as block:
                @block.sync
                def _(sp):
                    def stack(g, half):
                        q_cols = slice(half * HALF, (half + 1) * HALF)
                        k_cols = slice(WINDOW + half * HALF, WINDOW + (half + 1) * HALF)
                        sp.wait_ge(S["slots_ready"], 4 * (2 * g + half + 1))
                        sp.wait_ge(S["piece3_ready"], 2 * (2 * g + half + 1))
                        for h in range(HG):
                            sp.dma_start(q_stack[g % 2][0:KROWS, h, q_cols],
                                         piece[half][HD * h:HD * (h + 1), 0:TERMS, :]).then_inc(stack_sem(g, half), 16)
                            sp.dma_start(k_stack[g % 2][0:KROWS, h, k_cols],
                                         piece[half][HD * (HG + h):HD * (HG + h + 1), 1:SLOTS, :])\
                              .then_inc(stack_sem(g, half), 16)

                    for half in range(2):
                        stack(0, half)
                    for k in range(STEPS):
                        for kind, n in events(k):
                            if kind == "MAX":
                                sp.wait_ge(S["max_piece"], 3 * n + 3)
                                for i in range(3):
                                    sp.dma_start(q_stack[n % 2][KROWS + i:KROWS + i + 1, :, :], neg_max[i][:, :])\
                                      .then_inc(S["max_stacked"], 16)
                            elif kind == "STACK":
                                g, half = n
                                if g >= 2:
                                    sp.wait_ge(S["b_full"], HG * (NT * (g - 2) + (NT if half else 9)))
                                stack(g, half)

                @block.tensor
                def _(pe):
                    used = [0]

                    def misc_bank():
                        if used[0]:
                            pe.wait_ge(S["misc_free"], used[0])
                        used[0] += 1

                    def qk(g, c, k):
                        if k == 0:
                            misc_bank()
                        product = pe.matmul(misc[:, :], wqk_sb[:, g, k, :], xnT[:, k, 512 * c:512 * (c + 1)],
                                            start=(k == 0), stop=(k == KC - 1))
                        if k == KC - 1:
                            product.then_inc(S["misc_full"], 1)

                    for c in range(4):
                        for k in range(KC):
                            qk(0, c, k)
                    for k in range(STEPS):
                        for kind, n in events(k):
                            if kind == "A":
                                n, h = n
                                g, t = divmod(n, NT)
                                if h == 0 and (t == 0 or t == 7):
                                    pe.wait_ge(stack_sem(g, int(t == 7)), stacked(g))
                                i = HG * n + h
                                if i >= len(a_ring):
                                    pe.wait_ge(S["a_free"], i - len(a_ring) + 1)
                                for s in range(4):
                                    q = P * t + SP * s
                                    last = pe.matmul(a_ring[i % len(a_ring)][SP * s:SP * (s + 1), 0:WIN],
                                                     q_stack[g % 2][0:KROWS, h, q:q + SP],
                                                     k_stack[g % 2][0:KROWS, h, q:q + WIN],
                                                     start=True, stop=True)
                                last.then_inc(S["a_full"], 1)
                            elif kind == "QK":
                                qk(*n)
                            elif kind == "MAX":
                                pe.wait_ge(S["a_free"], NT * HG * (n + 1))
                                misc_bank()
                                pe.transpose(misc[0:NT * HG, 0:P],
                                             row_max[:, n, :, :].rearrange("p h t -> p (h t)"), ident)\
                                  .then_inc(S["misc_full"], 1)
                            elif kind == "B":
                                n, h = n
                                g, j = divmod(n, NT)
                                c0, c1 = window(j)
                                if j == 0 and h == 0:
                                    pe.wait_ge(S["max_stacked"], MAX_STACKED * (g + 1))
                                i = HG * n + h
                                if i >= S_RING:
                                    pe.wait_ge(S["exp_ready"], i - S_RING + 1)
                                pe.matmul(s_banks[:, i % S_RING, c0:c1],
                                          k_stack[g % 2][:, h, WINDOW + P * j:WINDOW + P * (j + 1)],
                                          q_stack[g % 2][:, h, P * (j - 1) + c0:P * (j - 1) + c1],
                                          start=True, stop=True).then_inc(S["b_full"], 1)
                            elif kind == "PV":
                                g, i = divmod(n, NT)
                                pe.wait_ge(S["band_ready"], band_count(min(n + 1, NT * g + NT - 1)))
                                if n % 4 == 0 and n:
                                    pe.wait_ge(S["o_copied"], n // 4)
                                keys = [j for j in (i - 1, i, i + 1) if 0 <= j < NT]
                                for j in keys:
                                    for h in range(HG):
                                        head = HG * g + h
                                        last = pe.matmul(
                                            o_bank[SP * h:SP * (h + 1), P * (i % 4):P * (i % 4 + 1)],
                                            v_sb[:, j, VW * head:VW * head + SP],
                                            probs[:, j % 4, h, P * (i - j + 1):P * (i - j + 2)],
                                            start=(j == keys[0]), stop=(j == keys[-1]))
                                last.then_inc(S["pv_done"], 1)
                            elif kind == "TURN":
                                pe.wait_ge(S["o_copied"], n + 1)
                                misc_bank()
                                for i in range(4):
                                    last = pe.transpose(misc[:, P * i:P * (i + 1)], o_raw[:, P * i:P * (i + 1)],
                                                        ident)
                                last.then_inc(S["misc_full"], 1)

                @block.scalar
                def _(act):
                    used = [0]

                    turned = [0]

                    def piece1(g, c):
                        used[0] += 1
                        if g >= 1:
                            act.wait_ge(stack_sem(g - 1, c // 2), stacked(g - 1))
                        act.wait_ge(S["misc_full"], used[0])
                        act.activation(piece[c // 2][:, 0, 512 * (c % 2):512 * (c % 2 + 1)], misc[:, :], ACT.Copy)\
                           .then_inc(S["piece1_ready"], 1)

                    for c in range(4):
                        piece1(0, c)
                    for k in range(STEPS):
                        for kind, n in events(k):
                            if kind == "PIECE1":
                                piece1(*n)
                            elif kind == "MAX":
                                used[0] += 1
                                act.wait_ge(S["p0_arg_ready"], n + 1)
                                act.activation(p0[:, n, :, :], p0_arg[:, :, :], ACT.Exp,
                                               scale=LOGIT_SCALE).then_inc(S["p0_ready"], 1)
                            elif kind == "B":
                                n, h = n
                                g, j = divmod(n, NT)
                                c0, c1 = window(j)
                                if n >= 4 and h == 0:
                                    act.wait_ge(S["pv_done"], n - 2)
                                i = HG * n + h
                                act.wait_ge(S["b_full"], i + 1)
                                act.activation(probs[:, j % 4, h, c0:c1], s_banks[:, i % S_RING, c0:c1],
                                               ACT.Exp, scale=LOGIT_SCALE).then_inc(S["exp_ready"], 1)
                            elif kind == "COPY_OUT":
                                act.wait_ge(S["pv_done"], 4 * n + 4)
                                if n:
                                    act.wait_ge(S["misc_full"], turned[0])
                                act.activation(o_raw[:, :], o_bank[:, :], ACT.Copy).then_inc(S["o_copied"], 1)
                            elif kind == "TURN":
                                used[0] += 1
                                turned[0] = used[0]

                @block.gpsimd
                def _(pool):
                    def piece3(g, c):
                        n = 4 * g + c
                        if g >= 1:
                            pool.wait_ge(stack_sem(g - 1, c // 2), stacked(g - 1))
                        pool.wait_ge(S["piece2_ready"], n + 1)
                        cols = slice(512 * (c % 2), 512 * (c % 2 + 1))
                        pool.tensor_tensor(piece[c // 2][:, SLOT_PIECE3, cols], rest[:, c % 2, :],
                                           piece[c // 2][:, SLOT_PIECE2, cols], ALU.subtract)\
                            .then_inc(S["piece3_ready"], 1)

                    for c in range(4):
                        piece3(0, c)
                    for k in range(STEPS):
                        for kind, n in events(k):
                            if kind == "SPLIT":
                                piece3(*n)
                            elif kind == "CUT":
                                g, j = divmod(n, NT)
                                pool.wait_ge(S["exp_ready"], HG * (n + 1))
                                if j > 0:
                                    part = probs[:, j % 4, :, 0:P]
                                    pool.affine_select(out=part, in_=part, compare_op=ALU.is_ge, fill=0.0,
                                                       base=0, pattern=[[0, HG], [1, P]],
                                                       channel_multiplier=-1).then_inc(S["band_ready"], 1)
                                if j < NT - 1:
                                    part = probs[:, j % 4, :, 2 * P:3 * P]
                                    pool.affine_select(out=part, in_=part, compare_op=ALU.is_ge, fill=0.0,
                                                       base=0, pattern=[[0, HG], [-1, P]],
                                                       channel_multiplier=1).then_inc(S["band_ready"], 1)
                            elif kind == "GLOB":
                                g, quartet = divmod(n, 4)
                                pool.wait_ge(S["p0_ready"], g + 1)
                                if n:
                                    pool.wait_ge(S["o_added"], n)
                                pool.tensor_tensor(
                                    glob_term[:, :, :, :],
                                    v0_all[:, VW * HG * g:VW * HG * (g + 1)]
                                    .rearrange("p (o h c) -> p o h c", o=1, c=VW).to_broadcast([P, 4, HG, VW]),
                                    p0[:, g, 4 * quartet:4 * quartet + 4, :].unsqueeze(3)
                                    .to_broadcast([P, 4, HG, VW]), ALU.mult).then_inc(S["glob_ready"], 1)

                @block.vector
                def _(dve):
                    used = [0]

                    def split(g, c):
                        n = 4 * g + c
                        used[0] += 1
                        half = piece[c // 2]
                        cols = slice(512 * (c % 2), 512 * (c % 2 + 1))
                        dve.wait_ge(S["piece1_ready"], n + 1)
                        if n >= 2:
                            dve.wait_ge(S["piece3_ready"], n - 1)
                        dve.tensor_tensor(rest[:, c % 2, :], misc[:, :], half[:, 0, cols], ALU.subtract)\
                           .then_inc(S["misc_free"], 1)
                        if g >= 1:
                            dve.wait_ge(stack_sem(g - 1, c // 2), stacked(g - 1))
                        dve.wait_ge(S["misc_free"], used[0])
                        dve.tensor_copy(half[:, SLOT_PIECE2, cols], rest[:, c % 2, :]).then_inc(S["piece2_ready"], 1)

                    def fill_slots(g, half, copies):
                        n = 2 * g + half
                        dve.wait_ge(S["piece2_ready"], 2 * n + 2)
                        for i in copies:
                            to, frm = ((1, 0), (4, 0), (6, 0), (3, SLOT_PIECE2))[i]
                            dve.tensor_copy(piece[half][:, to, :], piece[half][:, frm, :])\
                               .then_inc(S["slots_ready"], 1)

                    for c in range(4):
                        split(0, c)
                        if c % 2:
                            fill_slots(0, c // 2, range(4))
                    for k in range(STEPS):
                        for kind, n in events(k):
                            if kind == "A":
                                n, h = n
                                g, t = divmod(n, NT)
                                mask = band[0 if t == 0 else 2 if t == NT - 1 else 1]
                                i = HG * n + h
                                dve.wait_ge(S["a_full"], i + 1)
                                dve.tensor_tensor_reduce(
                                    out=a_ring[i % len(a_ring)][:, 0:WIN], in0=a_ring[i % len(a_ring)][:, 0:WIN], in1=mask,
                                    scale=1.0, scalar=s0T[:, t, HG * g + h:HG * g + h + 1], op0=ALU.add,
                                    op1=ALU.max, accum_out=row_max[:, g, h, t:t + 1]).then_inc(S["a_free"], 1)
                            elif kind == "SPLIT":
                                split(*n)
                            elif kind == "SLOTS":
                                fill_slots(*n)
                            elif kind == "MAX":
                                used[0] += 1
                                if n:
                                    dve.wait_ge(S["max_stacked"], MAX_STACKED * n)
                                    dve.wait_ge(S["p0_ready"], n)
                                dve.wait_ge(S["misc_full"], used[0])
                                turned = misc[0:NT * HG, 0:P]
                                dve.tensor_scalar(neg_max[0][:, :], turned, -1.0, None, ALU.mult)\
                                   .then_inc(S["max_piece"], 1)
                                dve.wait_ge(S["a_free"], NT * HG * (n + 1))
                                dve.tensor_tensor(
                                    p0_arg[:, 1:NT, :], s0T[:, 1:NT, HG * n:HG * n + HG],
                                    row_max[:, n, :, 1:NT].rearrange("p h t -> p t h"), ALU.subtract)\
                                   .then_inc(S["p0_diff"], 1)
                                dve.memset(p0_arg[:, 0, :], MASKED)
                                dve.wait_ge(S["p0_diff"], n + 1)
                                dve.memset(p0_arg[0:1, 1, :], MASKED).then_inc(S["p0_arg_ready"], 1)
                                dve.wait_ge(S["max_piece"], 3 * n + 1)
                                dve.scalar_tensor_tensor(out=neg_rest[:, :], in0=turned, scalar=-1.0,
                                                         in1=neg_max[0][:, :], op0=ALU.mult, op1=ALU.subtract)\
                                   .then_inc(S["misc_free"], 1)
                                dve.wait_ge(S["misc_free"], used[0])
                                dve.tensor_copy(neg_max[1][:, :], neg_rest[:, :]).then_inc(S["max_piece"], 1)
                                dve.wait_ge(S["max_piece"], 3 * n + 2)
                                dve.tensor_tensor(neg_max[2][:, :], neg_rest[:, :], neg_max[1][:, :],
                                                  ALU.subtract).then_inc(S["max_piece"], 1)
                            elif kind == "OUT":
                                g, quartet = divmod(n, 4)
                                used[0] += 1
                                dve.wait_ge(S["misc_full"], used[0])
                                dve.wait_ge(S["glob_ready"], n + 1)
                                if n:
                                    dve.wait_ge(S["attn_ready"], n)
                                dve.tensor_tensor(
                                    o_add[:, :, :, :].rearrange("p t h c -> p (t h) c"),
                                    misc[:, :].rearrange("p (th c) -> p th c", c=SP)[:, :, 0:VW],
                                    glob_term[:, :, :, :].rearrange("p t h c -> p (t h) c"), ALU.add)\
                                   .then_inc(S["o_added"], 1)
                                dve.wait_ge(S["o_added"], n + 1)
                                dve.reciprocal(recip[:, :, :], o_add[:, :, :, HD]).then_inc(S["misc_free"], 1)
                                dve.wait_ge(S["misc_free"], used[0])
                                dve.tensor_tensor(
                                    attn[:, 4 * quartet:4 * quartet + 4, HG * HD * g:HG * HD * (g + 1)]
                                    .rearrange("p t (h c) -> p t h c", c=HD),
                                    o_add[:, :, :, 0:HD],
                                    recip[:, :, :].unsqueeze(3).to_broadcast([P, 4, HG, HD]), ALU.mult)\
                                   .then_inc(S["attn_ready"], 1)
                    dve.wait_ge(S["attn_ready"], A_STEPS // 4)
                    dve.tensor_copy(attn[0:1, 0, :], o0_norm.rearrange("p h c -> p (h c)"))
            reset()

        with nc.Fori(0, B) as b:
            norm_block(NT, load=load_batch(x, b), gate_to=lambda: logits[:, bass.ds(b * NT, NT), :])
        first_any = route()
        with nc.If(first_any != 0):
            experts(x, x1)

        with nc.Block() as block:
            @block.gpsimd
            def _(pool):
                for s in range(2):
                    pool.memset(q_stack[s][KROWS:P, :, :], 0.0).then_inc(S["pool_step"], 1)
                    pool.memset(k_stack[s][KROWS:P, :, :], 0.0).then_inc(S["pool_step"], 1)
                    pool.memset(k_stack[s][0:KROWS, :, 0:WINDOW], 0.0).then_inc(S["pool_step"], 1)
                    pool.memset(k_stack[s][0:KROWS, :, WINDOW + T:], 0.0).then_inc(S["pool_step"], 1)
                pool.wait_ge(S["pool_step"], 8)
                pool.memset(k_stack[0][KROWS:KROWS + 3, :, :], 1.0).then_inc(S["pool_step"], 1)
                pool.memset(k_stack[1][KROWS:KROWS + 3, :, :], 1.0).then_inc(S["pool_step"], 1)
                pool.wait_ge(S["pool_step"], 10)


        reset()

        with nc.Fori(0, B) as b:
            def load(sp):
                with sp.If(first_any != 0):
                    load_batch(x1, b)(sp)
                with sp.Else():
                    load_batch(x, b)(sp)
            norm_block(NT, load=load, values=True)
            first_token_block()
            band_block()
            norm_block(NT, load=load, gate_to=lambda: logits[:, bass.ds(b * NT, NT), :], project=True,
                       store=lambda c: out[bass.ds(b, 1), 512 * c:512 * (c + 1), :]
                       .rearrange("o (t p) d -> p (o t) d", p=P))
        second_any = route()
        with nc.If(second_any != 0):
            experts(out, out)


def constants():
    import numpy as np
    con = np.zeros((P, C_END), np.float32)
    con[:, C_IDENT:C_IDENT + P] = np.eye(P)
    r = np.arange(P)[:, None] % SP
    strip = np.arange(P)[:, None] // SP
    c = np.arange(WIN)[None, :]
    outside = (c < r) | (c > 2 * WINDOW + r)
    key_first = SP * strip - WINDOW + c
    key_last = P * (NT - 1) + key_first
    for i, bad in enumerate((outside | (key_first < 0), outside, outside | (key_last >= T))):
        con[:, C_BAND + i * WIN:C_BAND + (i + 1) * WIN] = np.where(bad, MASKED, 0.0)
    pick = con[:, C_PICK:C_PICK + NG * SP].reshape(P, NG, SP)
    pick = np.zeros((P, NG, SP), np.float32)
    for p in range(P):
        for g in range(NG):
            half, row = divmod(p, HG * HD)
            pick[p, g, H * half + HG * g + row // HD] = 1.0
    con[:, C_PICK:C_PICK + NG * SP] = pick.reshape(P, -1)
    diag = np.zeros((P, H, VW), np.float32)
    for p in range(P):
        if p % SP < H:
            diag[p, p % SP, :] = 1.0
    con[:, C_DIAG:C_DIAG + H * VW] = diag.reshape(P, -1)
    con[:, C_RANK:C_RANK + E] = E - np.arange(E)
    return con


def chunked(w):
    return w.reshape(w.shape[0] // P, P, w.shape[1]).transpose(1, 0, 2)


def kernel(**inputs):
    import numpy as np
    import concourse.bacc as bacc
    from concourse.bass_utils import run_bass_kernel_spmd

    a = {k.replace("L0_", ""): np.asarray(v) for k, v in inputs.items()}
    wq, wk = a["attn_Wq"], a["attn_Wk"]
    n = HG * HD
    wqk = np.stack([np.concatenate([chunked(wq.T)[:, :, g * n:(g + 1) * n], chunked(wk.T)[:, :, g * n:(g + 1) * n]],
                                   axis=2) for g in range(NG)], axis=1)
    wback = np.stack([np.concatenate([wk[g * n:(g + 1) * n], wq[g * n:(g + 1) * n]], axis=0)
                      for g in range(NG)], axis=1)
    laid = {
        "x": a["attn_x"], "wqk": wqk, "wback": wback, "wv": chunked(a["attn_Wv"].T), "wo": chunked(a["attn_Wo"].T),
        "gate": chunked(a["ffn_gate_w"].T),
        "w1": np.stack([chunked(a["ffn_w1"][e].T) for e in range(E)]),
        "b1": a["ffn_b1"].reshape(E, KC, P).transpose(0, 2, 1),
        "w2": np.stack([chunked(a["ffn_w2"][e].T) for e in range(E)]),
        "b2": a["ffn_b2"], "consts": constants(),
    }
    nc = bacc.Bacc("TRN2", target_bir_lowering=False, num_devices=1)
    arrays, args = {}, {}
    for name, array in laid.items():
        arrays[f"in_{name}"] = np.ascontiguousarray(array)
        args[name] = nc.dram_tensor(f"in_{name}", array.shape, FP32, kind="ExternalInput").ap()
    x1 = nc.dram_tensor("x1_scratch", (B, T, D), FP32, kind="Internal").ap()
    out = nc.dram_tensor("out_x", (B, T, D), FP32, kind="ExternalOutput").ap()
    build(nc, x1=x1, out=out, **args)
    r = run_bass_kernel_spmd(nc, [arrays], core_ids=[0])
    return r.results[0]["out_x"]
```

```python
import concourse.bass as bass
from concourse import mybir
from contextlib import ExitStack

FP32 = mybir.dt.float32
BF16 = mybir.dt.bfloat16
I32 = mybir.dt.int32
ALU = mybir.AluOpType
ACT = mybir.ActivationFunctionType
AX = mybir.AxisListType

B, T, D = 4, 2048, 256
H, HD = 16, 16
E = 8
N = B * T
CAPACITY = int(1.25 * N / E)
EPS = 1e-5
LOGIT_SCALE = 0.25
WINDOW = 128

P = 128
NT = T // P
KC = D // P
HG = 4
NG = H // HG
SP = 32
VW = HD + 1
WIN = 2 * WINDOW + SP
TERMS = 6
SLOTS = TERMS + 1
SLOT_PIECE2, SLOT_PIECE3 = 2, 5
KROWS = HD * TERMS
HALF = T // 2
MASKED = -1.0e30

C_IDENT = 0
C_BAND = C_IDENT + P
C_PICK = C_BAND + 3 * WIN
C_DIAG = C_PICK + NG * SP
C_RANK = C_DIAG + H * VW
C_LOWEST = C_RANK + E
C_END = C_LOWEST + 1


def build(nc, x, wqk, wback, wv, wo, gate, w1, b1, w2, b2, consts, x1, out):
    ctx = ExitStack()
    with ctx:
        def sb(name, shape, dt=FP32):
            return ctx.enter_context(nc.sbuf_tensor(name, shape, dt))

        q_stack = [sb(f"q_stack{i}", [P, HG, T], BF16) for i in range(2)]
        k_stack = [sb(f"k_stack{i}", [P, HG, T + 2 * WINDOW], BF16) for i in range(2)]
        xnT = sb("xnT", [P, KC, T])
        v_sb = sb("v_sb", [P, NT, H * VW + SP - VW])
        probs = sb("probs", [P, 4, HG, 3 * P])
        attn = sb("attn", [P, NT, D])
        x_b = sb("x_b", [P, NT, D])
        piece0 = sb("piece0", [P, SLOTS, HALF], BF16)
        rest = sb("rest", [P, 2, 512])
        wqk_sb = sb("wqk_sb", [P, NG, KC, P])
        wback_sb = sb("wback_sb", [P, NG, D])
        wv_sb = sb("wv_sb", [P, KC, D])
        wo_sb = sb("wo_sb", [P, KC, D])
        gate_sb = sb("gate_sb", [P, KC, SP])
        con = sb("con", [P, C_END])
        ones = sb("ones", [P, P])
        neg_half = sb("neg_half", [P, 4])
        v0_all = sb("v0_all", [P, H * VW])
        o_raw = sb("o_raw", [P, 4 * P])
        o_add = sb("o_add", [P, 4, HG, VW])
        glob_term = sb("glob_term", [P, 4, HG, VW])
        recip = sb("recip", [P, 4, HG])
        s0T = sb("s0T", [P, NT, H])
        row_max = sb("row_max", [P, NG, HG, NT])
        p0_arg = sb("p0_arg", [P, NT, HG])
        p0 = sb("p0", [P, NG, NT, HG])
        neg_max = [sb(f"neg_max{i}", [NT * HG, P], BF16) for i in range(3)]
        neg_rest = sb("neg_rest", [NT * HG, P])
        logits = sb("logits", [P, B * NT, E])
        stats = sb("stats", [P, 4, 6])
        mean_var = sb("mean_var", [P, NT, 2])
        var_eps = sb("var_eps", [P, NT])
        rstd = sb("rstd", [P, NT])
        small = sb("small", [P, 64])
        flags = sb("flags", [1, E + 1], I32)

        probs_flat = probs[:, :, :, :].rearrange("p a h n -> p (a h n)")
        attn_flat = attn[:, :, :].rearrange("p t d -> p (t d)")
        piece = [piece0[:, :, :], x_b[:, :, :].rearrange("p t d -> p (t d)").bitcast(BF16)
                 [:, 0:SLOTS * HALF].rearrange("p (s n) -> p s n", s=SLOTS)]
        o0_norm = x_b[0:1, NT - 1, :].rearrange("p (h c) -> p h c", c=HD)
        xn = probs_flat[:, 0:8 * D].rearrange("p (t d) -> p t d", t=8)
        attnT = probs_flat[:, 2048:3072].rearrange("p (s k n) -> p s k n", s=2, k=KC)
        strip_rows = probs_flat[:, 3072:3584]
        sg_arg = probs_flat[:, 3584:3840].rearrange("p (m h) -> p m h", h=H)
        masked_o0 = probs_flat[:, 3840:3840 + H * VW]
        o0_row = probs_flat[0:1, 4112:4112 + H * VW]
        pgT = probs_flat[:, 4400:4400 + NT * SP].rearrange("p (m c) -> p m c", c=SP)
        uw = probs_flat[:, 4912:4912 + KC * SP].rearrange("p (k c) -> p k c", k=KC)
        first_scaled = probs_flat[:, 4976:4976 + NG * SP].rearrange("p (g c) -> p g c", g=NG)
        wts = rest[:, 0, :].rearrange("p (t e) -> p t e", e=E)
        ident = con[:, C_IDENT:C_IDENT + P]
        band = [con[:, C_BAND + i * WIN:C_BAND + (i + 1) * WIN] for i in range(3)]
        pick = con[:, C_PICK:C_PICK + NG * SP].rearrange("p (g c) -> p g c", g=NG)
        diag = con[:, C_DIAG:C_DIAG + H * VW]
        rank = con[:, C_RANK:C_RANK + E]
        v_heads = v_sb[:, :, 0:H * VW].rearrange("p t (h c) -> p t h c", c=VW)

        bank = [ctx.enter_context(nc.psum_tensor(f"bank{i}", [P, 512], FP32)) for i in range(2)]
        s_banks = ctx.enter_context(nc.psum_tensor("s_banks", [P, 4, 512], FP32))
        o_bank = ctx.enter_context(nc.psum_tensor("o_bank", [P, 512], FP32))
        misc = ctx.enter_context(nc.psum_tensor("misc", [P, 512], FP32))
        a_ring = [bank[0], bank[1], s_banks[:, 3, :]]
        S_RING = 3

        names = ["x_in0", "x_in1", "x_in2", "x_in3", "consts_in", "filled", "stats_ready", "moments_ready",
                 "eps_added", "rstd_ready", "xn_ready", "xnT_psum", "xnT_ready", "v_psum", "v_ready",
                 "gate_psum", "gate_rows", "gate_cols", "logits_ready",
                 "proj_in_psum", "proj_in_sbuf", "proj_psum", "x2_ready", "stored",
                 "pe_step", "dve_step", "act_step", "pool_step",
                 "misc_full", "misc_free", "piece1_ready", "piece2_ready", "piece3_ready", "slots_ready",
                 "stack00", "stack01", "stack10", "stack11", "a_full", "a_free",
                 "max_piece", "max_stacked", "max_ready", "p0_diff", "p0_arg_ready", "p0_ready",
                 "b_full", "exp_ready", "band_ready", "pv_done", "o_copied", "glob_ready", "o_added",
                 "attn_ready"]
        sems = {n: ctx.enter_context(nc.semaphore(n)) for n in names}
        nums = [s.num for s in sems.values()]
        assert max(nums) - min(nums) + 1 == len(nums)
        S = sems

        def reset():
            nc.all_engine_barrier(sems_to_clear=range(min(nums), max(nums) + 1))

        with nc.Block() as block:
            @block.sync
            def _(sp):
                for dst, src in ((con[:, :], consts), (wqk_sb[:, :, :, :], wqk), (wback_sb[:, :, :], wback),
                                 (wv_sb[:, :, :], wv), (wo_sb[:, :, :], wo), (gate_sb[:, :, 0:E], gate)):
                    sp.dma_start(dst, src).then_inc(S["consts_in"], 16)
                sp.wait_ge(S["consts_in"], 6 * 16)

            @block.vector
            def _(dve):
                dve.memset(ones[:, :], 1.0)
                dve.memset(neg_half[:, :], -0.5)
                dve.memset(gate_sb[:, :, E:SP], 0.0)
                def zero(stack, rows, cols):
                    return dve.memset(stack[rows, :, :].bitcast(FP32)[:, :, cols], 0.0)

                for s in range(2):
                    zero(k_stack[s], slice(KROWS, P), slice(0, (T + 2 * WINDOW) // 2)).then_inc(S["filled"], 1)
                for s in range(2):
                    zero(q_stack[s], slice(KROWS, P), slice(0, T // 2))
                    zero(k_stack[s], slice(0, KROWS), slice(0, WINDOW // 2))
                    zero(k_stack[s], slice(0, KROWS), slice((WINDOW + T) // 2, T // 2 + WINDOW))

            @block.gpsimd
            def _(pool):
                for s in range(2):
                    pool.wait_ge(S["filled"], s + 1)
                    pool.memset(k_stack[s][KROWS:KROWS + 3, :, :], 1.0)
        reset()

        def norm_block(ntiles, load=None, gate_to=None, project=False, store=None):
            chunks = ntiles // 4
            pairs = ntiles // 2
            with nc.Block() as block:
                @block.sync
                def _(sp):
                    if load:
                        load(sp)
                    if store:
                        for c in range(chunks):
                            sp.wait_ge(S["x2_ready"], 2 * c + 2)
                            sp.dma_start(store(c), x_b[:, 4 * c:4 * c + 4, :]).then_inc(S["stored"], 16)
                        sp.wait_ge(S["stored"], 16 * chunks)

                @block.vector
                def _(dve):
                    def normalise(c):
                        dve.wait_ge(S["rstd_ready"], c + 1)
                        if c >= 2:
                            dve.wait_ge(S["xnT_psum"], 2 * c - 2)
                        for t in range(4 * c, 4 * c + 4):
                            dve.tensor_scalar(xn[:, t % 8, :], x_b[:, t, :], mean_var[:, t, 0:1],
                                              rstd[:, t:t + 1], ALU.subtract, ALU.mult)\
                               .then_inc(S["xn_ready"], 1)

                    for c in range(chunks):
                        if project:
                            dve.wait_ge(S[f"x_in{c}"], 16)
                            for u in (2 * c, 2 * c + 1):
                                dve.wait_ge(S["proj_psum"], u + 1)
                                dve.tensor_tensor(
                                    x_b[:, 2 * u:2 * u + 2, :],
                                    s_banks[:, 2 + u % 2, :].rearrange("p (t d) -> p t d", t=2),
                                    x_b[:, 2 * u:2 * u + 2, :], ALU.add).then_inc(S["x2_ready"], 1)
                            dve.wait_ge(S["x2_ready"], 2 * c + 2)
                        else:
                            dve.wait_ge(S[f"x_in{c}"], 16)
                        if c:
                            dve.wait_ge(S["moments_ready"], 4 * c)
                        for t in range(4 * c, 4 * c + 4):
                            dve.bn_stats(stats[:, t % 4, :], x_b[:, t, :]).then_inc(S["stats_ready"], 1)
                        for t in range(4 * c, 4 * c + 4):
                            dve.wait_ge(S["stats_ready"], t + 1)
                            dve.bn_aggr(mean_var[:, t, :], stats[:, t % 4, :]).then_inc(S["moments_ready"], 1)
                        if c >= 1:
                            normalise(c - 1)
                    normalise(chunks - 1)
                    if gate_to is not None:
                        dve.wait_ge(S["gate_cols"], 1)
                        if ntiles == NT:
                            dve.tensor_copy(
                                gate_to().rearrange("p (g c) e -> p g c e", g=4),
                                s_banks[:, 3, :].rearrange("p (c g e) -> p g c e", c=4, g=4)[:, :, :, 0:E])\
                               .then_inc(S["logits_ready"], 1)

                @block.gpsimd
                def _(pool):
                    for c in range(chunks):
                        pool.wait_ge(S["moments_ready"], 4 * c + 4)
                        pool.tensor_scalar(var_eps[:, 4 * c:4 * c + 4], mean_var[:, 4 * c:4 * c + 4, 1],
                                           EPS, None, ALU.add).then_inc(S["eps_added"], 1)
                        pool.wait_ge(S["eps_added"], c + 1)
                        pool.tensor_tensor(rstd[:, 4 * c:4 * c + 4], var_eps[:, 4 * c:4 * c + 4],
                                           neg_half[:, :], ALU.pow).then_inc(S["rstd_ready"], 1)

                @block.scalar
                def _(act):
                    def take_attnT(u):
                        act.wait_ge(S["proj_in_psum"], u + 1)
                        if u >= 2:
                            act.wait_ge(S["proj_psum"], u - 1)
                        act.activation(attnT[:, u % 2, :, :],
                                       s_banks[:, u % 2, :].rearrange("p (k n) -> p k n", k=KC),
                                       ACT.Copy).then_inc(S["proj_in_sbuf"], 1)

                    def take_xnT(u):
                        act.wait_ge(S["xnT_psum"], u + 1)
                        act.activation(xnT[:, :, 2 * P * u:2 * P * (u + 1)],
                                       bank[u % 2][:, :].rearrange("p (k n) -> p k n", k=KC),
                                       ACT.Copy).then_inc(S["xnT_ready"], 1)

                    for c in range(chunks + 2):
                        if project and c < chunks:
                            take_attnT(2 * c)
                            take_attnT(2 * c + 1)
                        if c >= 2:
                            take_xnT(2 * c - 4)
                            take_xnT(2 * c - 3)
                    if gate_to is not None:
                        act.wait_ge(S["gate_psum"], 1)
                        act.activation(strip_rows, misc[:, :], ACT.Copy).then_inc(S["gate_rows"], 1)

                @block.tensor
                def _(pe):
                    def project_pair(u):
                        if u >= 2:
                            pe.wait_ge(S["proj_in_sbuf"], u - 1)
                        for k in range(KC):
                            for i in range(2):
                                last = pe.transpose(s_banks[:, u % 2, k * 2 * P + i * P:k * 2 * P + (i + 1) * P],
                                                    attn[:, 2 * u + i, k * P:(k + 1) * P], ident)
                        last.then_inc(S["proj_in_psum"], 1)

                    def project_out(u):
                        pe.wait_ge(S["proj_in_sbuf"], u + 1)
                        if u >= 2:
                            pe.wait_ge(S["x2_ready"], u - 1)
                        for i in range(2):
                            for k in range(KC):
                                last = pe.matmul(s_banks[:, 2 + u % 2, i * D:(i + 1) * D],
                                                 attnT[:, u % 2, k, i * P:(i + 1) * P], wo_sb[:, k, :],
                                                 start=(k == 0), stop=(k == KC - 1))
                        last.then_inc(S["proj_psum"], 1)

                    def transpose_pair(u):
                        pe.wait_ge(S["xn_ready"], 2 * u + 2)
                        if u >= 2:
                            pe.wait_ge(S["xnT_ready"], u - 1)
                        for k in range(KC):
                            for i in range(2):
                                last = pe.transpose(bank[u % 2][:, k * 2 * P + i * P:k * 2 * P + (i + 1) * P],
                                                    xn[:, (2 * u + i) % 8, k * P:(k + 1) * P], ident)
                        last.then_inc(S["xnT_psum"], 1)

                    for c in range(chunks + 2):
                        if project and c < chunks:
                            for u in (2 * c, 2 * c + 1):
                                project_pair(u)
                                if u >= 1:
                                    project_out(u - 1)
                            project_out(2 * c + 1) if c == chunks - 1 else None
                        if c >= 2:
                            transpose_pair(2 * c - 4)
                            transpose_pair(2 * c - 3)
                    if gate_to is not None:
                        pe.wait_ge(S["xnT_ready"], pairs)
                        for k in range(KC):
                            for g in range(4):
                                last = pe.matmul(misc[SP * g:SP * (g + 1), :], gate_sb[:, k, :],
                                                 xnT[:, k, 512 * g:512 * (g + 1)],
                                                 start=(k == 0), stop=(k == KC - 1))
                        last.then_inc(S["gate_psum"], 1)
                        pe.wait_ge(S["gate_rows"], 1)
                        if project:
                            pe.wait_ge(S["x2_ready"], pairs)
                        for c in range(4):
                            last = pe.transpose(s_banks[:, 3, P * c:P * (c + 1)],
                                                strip_rows[:, P * c:P * (c + 1)], ident)
                        last.then_inc(S["gate_cols"], 1)
            reset()

        def load_batch(dram, b):
            def load(sp):
                for c in range(NT // 4):
                    sp.dma_start(x_b[:, 4 * c:4 * c + 4, :],
                                 dram[bass.ds(b, 1), 512 * c:512 * (c + 1), :]
                                 .rearrange("o (t p) d -> p (o t) d", p=P)).then_inc(S[f"x_in{c}"], 16)
            return load

        def route():
            L = B * NT
            tmp = [attn_flat[:, i * 512:(i + 1) * 512].rearrange("p (t e) -> p t e", e=E) for i in range(6)]
            row = [attn_flat[:, 3072 + i * L:3072 + (i + 1) * L] for i in range(4)]
            counts = attn_flat[:, 3600:3600 + E]
            keep = attn_flat[:, 3616:3616 + E + 1]

            def wide(r):
                return r.unsqueeze(2).to_broadcast([P, L, E])

            rank_all = rank.unsqueeze(1).to_broadcast([P, L, E])
            with nc.Block() as block:
                @block.vector
                def _(dve):
                    done = [0]

                    def step(ins):
                        done[0] += 1
                        ins.then_inc(S["dve_step"], 1)
                        dve.wait_ge(S["dve_step"], done[0])

                    step(dve.tensor_reduce(row[0], logits[:, :, :], AX.X, ALU.max))
                    step(dve.tensor_tensor(tmp[0], logits[:, :, :], wide(row[0]), ALU.subtract))
                    dve.wait_ge(S["act_step"], 1)
                    step(dve.tensor_reduce(row[1], tmp[1], AX.X, ALU.add))
                    step(dve.reciprocal(row[2], row[1]))
                    probs_e = tmp[0]
                    step(dve.tensor_tensor(probs_e, tmp[1], wide(row[2]), ALU.mult))

                    def pick_first_largest(values, selected, a):
                        step(dve.tensor_reduce(row[0], values, AX.X, ALU.max))
                        step(dve.tensor_tensor(a, values, wide(row[0]), ALU.is_equal))
                        step(dve.tensor_tensor(a, a, rank_all, ALU.mult))
                        step(dve.tensor_reduce(row[1], a, AX.X, ALU.max))
                        step(dve.tensor_tensor(selected, rank_all, wide(row[1]), ALU.is_equal))

                    pick_first_largest(probs_e, tmp[2], tmp[1])
                    step(dve.scalar_tensor_tensor(out=tmp[3], in0=tmp[2], scalar=-4.0, in1=probs_e,
                                                  op0=ALU.mult, op1=ALU.add))
                    pick_first_largest(tmp[3], tmp[4], tmp[1])
                    step(dve.tensor_tensor(tmp[2], tmp[2], tmp[4], ALU.add))
                    step(dve.tensor_reduce(counts, tmp[2].rearrange("p t e -> p e t"), AX.X, ALU.add))
                    dve.wait_ge(S["pe_step"], 1)
                    step(dve.tensor_scalar(keep[:, 0:E], misc[:, 0:E], float(CAPACITY), None, ALU.is_le))
                    step(dve.tensor_reduce(keep[:, E:E + 1], keep[:, 0:E], AX.X, ALU.max))
                    step(dve.tensor_copy(flags[0:1, :], keep[0:1, :]))
                    step(dve.tensor_tensor(tmp[3], tmp[2], probs_e, ALU.mult))
                    step(dve.scalar_tensor_tensor(out=wts[:, :, :], in0=tmp[3], scalar=0.5,
                                                  in1=keep[:, 0:E].unsqueeze(1).to_broadcast([P, L, E]),
                                                  op0=ALU.mult, op1=ALU.mult))

                @block.scalar
                def _(act):
                    act.wait_ge(S["dve_step"], 2)
                    act.activation(tmp[1], tmp[0], ACT.Exp).then_inc(S["act_step"], 1)

                @block.tensor
                def _(pe):
                    pe.wait_ge(S["dve_step"], 18)
                    pe.matmul(misc[:, 0:E], ones[:, :], counts, start=True, stop=True)\
                      .then_inc(S["pe_step"], 1)
            reset()
            return nc.values_load(flags[0:1, E:E + 1], min_val=0, max_val=1)

        def experts(src, dst):
            pool_w = v_sb[:, :, :].rearrange("p t c -> p (t c)")
            w1_sb = pool_w[:, 0:KC * D].rearrange("p (k n) -> p k n", k=KC)
            w2_sb = pool_w[:, 512:512 + KC * D].rearrange("p (k n) -> p k n", k=KC)
            b1_sb = pool_w[:, 1024:1024 + KC]
            b2_sb = pool_w[0:1, 1280:1280 + D]
            hT = pool_w[:, 1536:1536 + KC * 512].rearrange("p (k n) -> p k n", k=KC)
            weight = pool_w[:, 2600:2604]

            def chunk_of(dram, c):
                return dram.rearrange("b t d -> (b t) d").rearrange("(c t p) d -> c p t d", t=4, p=P)[
                    bass.ds(c, 1)].rearrange("o p t d -> p (o t) d")

            with nc.Fori(0, N // 512) as c:
                norm_block(4, load=lambda sp: sp.dma_start(x_b[:, 0:4, :], chunk_of(src, c))
                           .then_inc(S["x_in0"], 16))
                with nc.Fori(0, E) as e:
                    kept = nc.values_load(flags[0:1, bass.ds(e, 1)], min_val=0, max_val=1)
                    with nc.If(kept != 0):
                        with nc.Block() as block:
                            @block.sync
                            def _(sp):
                                for to, frm in ((w1_sb, w1[bass.ds(e, 1)].rearrange("o p k n -> p (o k) n")),
                                                (w2_sb, w2[bass.ds(e, 1)].rearrange("o p k n -> p (o k) n")),
                                                (b1_sb, b1[bass.ds(e, 1)].rearrange("o p k -> p (o k)")),
                                                (b2_sb, b2[bass.ds(e, 1), :])):
                                    sp.dma_start(to, frm).then_inc(S["consts_in"], 16)

                            @block.tensor
                            def _(pe):
                                pe.wait_ge(S["consts_in"], 64)
                                for f in range(KC):
                                    for k in range(KC):
                                        last = pe.matmul(bank[f][:, :], w1_sb[:, k, f * P:(f + 1) * P],
                                                         xnT[:, k, 0:512], start=(k == 0), stop=(k == KC - 1))
                                    last.then_inc(S["pe_step"], 1)
                                pe.wait_ge(S["act_step"], 2 * KC)
                                for t in range(4):
                                    o = s_banks[:, t, 0:D]
                                    for k in range(KC):
                                        pe.matmul(o, hT[:, k, t * P:(t + 1) * P], w2_sb[:, k, :],
                                                  start=(k == 0), stop=False)
                                    pe.matmul(o, ones[0:1, :], b2_sb, start=False, stop=True)\
                                      .then_inc(S["pe_step"], 1)

                            @block.scalar
                            def _(act):
                                act.wait_ge(S["consts_in"], 64)
                                for f in range(KC):
                                    act.wait_ge(S["pe_step"], f + 1)
                                    act.activation(hT[:, f, :], bank[f][:, :], ACT.Silu,
                                                   bias=b1_sb[:, f:f + 1]).then_inc(S["act_step"], 2)

                            @block.gpsimd
                            def _(pool):
                                pool.tensor_copy(weight, wts[:, bass.ds(c * 4, 4), bass.ds(e, 1)]
                                                 .rearrange("p t o -> p (t o)")).then_inc(S["pool_step"], 1)

                            @block.vector
                            def _(dve):
                                dve.wait_ge(S["pool_step"], 1)
                                for t in range(4):
                                    dve.wait_ge(S["pe_step"], KC + t + 1)
                                    dve.scalar_tensor_tensor(out=x_b[:, t, :], in0=s_banks[:, t, 0:D],
                                                             scalar=weight[:, t:t + 1], in1=x_b[:, t, :],
                                                             op0=ALU.mult, op1=ALU.add)
                        reset()
                with nc.Block() as block:
                    @block.sync
                    def _(sp):
                        sp.dma_start(chunk_of(dst, c), x_b[:, 0:4, :]).then_inc(S["stored"], 16)
                        sp.wait_ge(S["stored"], 16)
                reset()

        A_STEPS = NG * NT
        LAG_B, LAG_PV, LAG_OUT = NT + 3, NT + 6, NT + 7
        STEPS = A_STEPS + LAG_OUT + 1
        QK_AT = {3: 0, 7: 1, 11: 2, 15: 3}
        FIRST_AT = (1, 2, 5, 6, 17, 18)
        SLOTS_AT = {9: (0, (0, 1)), 10: (0, (2, 3)), 17: (1, (0, 1)), 18: (1, (2, 3))}

        def band_count(n):
            g, j = divmod(n, NT)
            return g * (2 * NT - 2) + min(1 + 2 * j, 2 * NT - 2)

        def pv_count(n, part):
            g, i = divmod(n, NT)
            return g * (3 * NT - 2) + min(3 * i + part, 3 * NT - 2)

        def next_groups(k, at):
            return [g for g in range(1, NG) if k - NT * (g - 1) == at]

        def events(k):
            a, b = k < A_STEPS, 0 <= k - LAG_B < A_STEPS
            turn = 0 <= k - LAG_OUT < A_STEPS and (k - LAG_OUT) % 4 == 3
            quartet = (k - LAG_OUT) // 4
            for half, at in enumerate((12, 19)):
                for g in next_groups(k, at):
                    yield "STACK", (g, half)
            if k in FIRST_AT:
                yield "FIRST", FIRST_AT.index(k) + 3
            for h in range(HG):
                if a:
                    yield "A", (k, h)
                if 0 <= k - LAG_PV < A_STEPS:
                    for part in ((0, 1, 2) if a and h == 0 else () if a or h == 3 else (h,)):
                        if 0 <= (k - LAG_PV) % NT + part - 1 < NT:
                            yield "PV", (k - LAG_PV, part)
                if h == 0:
                    if turn:
                        yield "TURN", quartet
                    for at, c in QK_AT.items():
                        for g in next_groups(k, at + 1):
                            yield "PIECE1", (g, c)
                    if k > NT and k % NT == 1 and k <= A_STEPS + 1:
                        yield "KEY0", k // NT - 1
                if k < NT and h % 2:
                    yield "VALUES", (k // 2, 2 * (k % 2) + h // 2)
                if b:
                    yield "B", (k - LAG_B, h)
                if h == (1 if a else 3) and 0 <= k - LAG_PV < A_STEPS and (k - LAG_PV) % 4 == 3:
                    yield "COPY_OUT", (k - LAG_PV) // 4
                if h == 1 and turn:
                    yield "OUT", quartet
                if h == 1 and k > NT and k % NT == 1 and k <= A_STEPS + 1:
                    yield "MAX", k // NT - 1
                if h >= 2:
                    for at, c in QK_AT.items():
                        for g in next_groups(k, at):
                            yield "QK", (g, c, h - 2)
            if b:
                yield "CUT", k - LAG_B
            if 0 <= k + 1 - LAG_OUT < A_STEPS and (k + 1 - LAG_OUT) % 4 == 3:
                yield "GLOB", (k + 1 - LAG_OUT) // 4
            for at, c in QK_AT.items():
                for g in next_groups(k, at + 1):
                    yield "SPLIT", (g, c)
            for at, (half, copies) in SLOTS_AT.items():
                for g in next_groups(k, at):
                    yield "SLOTS", (g, half, copies)

        def window(j):
            return (P if j == 0 else 0), (2 * P if j == NT - 1 else 3 * P)

        STACK_DMAS = 2 * HG

        MAX_STACKED = 16 * 3

        def stack_sem(g, half):
            return S[f"stack{g % 2}{half}"]

        def stacked(g):
            return 16 * STACK_DMAS * (g // 2 + 1)

        def attention_block(load):
            with nc.Block() as block:
                @block.sync
                def _(sp):
                    load(sp)

                    def stack(g, half):
                        q_cols = slice(half * HALF, (half + 1) * HALF)
                        k_cols = slice(WINDOW + half * HALF, WINDOW + (half + 1) * HALF)
                        sp.wait_ge(S["slots_ready"], 4 * (2 * g + half + 1))
                        sp.wait_ge(S["piece3_ready"], 2 * (2 * g + half + 1))
                        for h in range(HG):
                            sp.dma_start(q_stack[g % 2][0:KROWS, h, q_cols],
                                         piece[half][HD * h:HD * (h + 1), 0:TERMS, :]).then_inc(stack_sem(g, half), 16)
                            sp.dma_start(k_stack[g % 2][0:KROWS, h, k_cols],
                                         piece[half][HD * (HG + h):HD * (HG + h + 1), 1:SLOTS, :])\
                              .then_inc(stack_sem(g, half), 16)

                    for half in range(2):
                        stack(0, half)
                    for k in range(STEPS):
                        for kind, n in events(k):
                            if kind == "MAX":
                                sp.wait_ge(S["max_piece"], 3 * n + 3)
                                for i in range(3):
                                    sp.dma_start(q_stack[n % 2][KROWS + i:KROWS + i + 1, :, :], neg_max[i][:, :])\
                                      .then_inc(S["max_stacked"], 16)
                            elif kind == "STACK":
                                g, half = n
                                if g >= 2:
                                    sp.wait_ge(S["b_full"], HG * (NT * (g - 2) + (NT if half else 9)))
                                stack(g, half)

                @block.tensor
                def _(pe):
                    used = [0]

                    def misc_bank():
                        if used[0]:
                            pe.wait_ge(S["misc_free"], used[0])
                        used[0] += 1

                    def qk(g, c, k):
                        if k == 0:
                            misc_bank()
                        product = pe.matmul(misc[:, :], wqk_sb[:, g, k, :], xnT[:, k, 512 * c:512 * (c + 1)],
                                            start=(k == 0), stop=(k == KC - 1))
                        if k == KC - 1:
                            product.then_inc(S["misc_full"], 1)

                    def transpose_pair(u):
                        pe.wait_ge(S["xn_ready"], 2 * u + 2)
                        if u >= 2:
                            pe.wait_ge(S["xnT_ready"], u - 1)
                        for k in range(KC):
                            for i in range(2):
                                last = pe.transpose(bank[u % 2][:, k * 2 * P + i * P:k * 2 * P + (i + 1) * P],
                                                    xn[:, (2 * u + i) % 8, k * P:(k + 1) * P], ident)
                        last.then_inc(S["xnT_psum"], 1)

                    def values(u, part):
                        i, k = divmod(part, KC)
                        if u >= 2 and part == 0:
                            pe.wait_ge(S["v_ready"], u - 1)
                        product = pe.matmul(s_banks[:, u % 2, i * D:(i + 1) * D],
                                            xnT[:, k, (2 * u + i) * P:(2 * u + i + 1) * P], wv_sb[:, k, :],
                                            start=(k == 0), stop=(k == KC - 1))
                        if part == 3:
                            product.then_inc(S["v_psum"], 1)

                    def first_token(stage):
                        if stage == 0:
                            for g in range(NG):
                                for k in range(KC):
                                    last = pe.matmul(o_bank[:, g:g + 1], wqk_sb[:, g, k, :], xnT[:, k, 0:1],
                                                     start=(k == 0), stop=(k == KC - 1))
                        elif stage == 1:
                            pe.wait_ge(S["dve_step"], NG)
                            for k in range(KC):
                                for g in range(NG):
                                    last = pe.matmul(o_bank[:, 64 + k * SP:64 + (k + 1) * SP],
                                                     wback_sb[:, g, k * P:(k + 1) * P], first_scaled[:, g, :],
                                                     start=(g == 0), stop=(g == NG - 1))
                        elif stage == 2:
                            pe.wait_ge(S["dve_step"], NG + 1)
                            for k in range(KC):
                                for g in range(4):
                                    last = pe.matmul(s_banks[SP * g:SP * (g + 1), 2, :], uw[:, k, :],
                                                     xnT[:, k, 512 * g:512 * (g + 1)],
                                                     start=(k == 0), stop=(k == KC - 1))
                        elif stage == 3:
                            pe.wait_ge(S["act_step"], 1)
                            for c in range(4):
                                last = pe.transpose(o_bank[:, P * c:P * (c + 1)],
                                                    strip_rows[:, P * c:P * (c + 1)], ident)
                        elif stage == 4:
                            pe.wait_ge(S["dve_step"], NG + 2)
                            last = pe.transpose(s_banks[0:1, 2, 128:256], small[:, 0:1], ident)
                        elif stage == 5:
                            pe.wait_ge(S["dve_step"], NG + 4)
                            last = pe.matmul(s_banks[:, 2, 256:256 + H], ones[0:1, :], small[0:1, 32:32 + H],
                                             start=True, stop=True)
                        elif stage == 6:
                            pe.wait_ge(S["dve_step"], NG + 5)
                            pe.wait_ge(S["pool_step"], 1)
                            pe.wait_ge(S["v_ready"], 1)
                            last = pe.matmul(s_banks[:, 2, 0:H * VW], ones[0:1, :], v_sb[0:1, 0, 0:H * VW],
                                             start=True, stop=True)
                        elif stage == 7:
                            pe.wait_ge(S["act_step"], 2)
                            pe.wait_ge(S["v_ready"], NT // 2)
                            for m in range(NT):
                                s = m // 4
                                tile = 4 * (m % 4) + m // 4
                                last = pe.matmul(o_bank[SP * s:SP * (s + 1), 0:H * VW], pgT[:, m, :],
                                                 v_sb[:, tile, 0:H * VW], start=(m % 4 == 0), stop=(m % 4 == 3))
                        elif stage == 8:
                            pe.wait_ge(S["dve_step"], NG + 8)
                            last = pe.matmul(s_banks[0:1, 2, 0:H * VW], ones[:, 0:1], masked_o0,
                                             start=True, stop=True)
                        last.then_inc(S["pe_step"], 1)

                    def first_qk(c):
                        pe.wait_ge(S["xnT_ready"], 2 * c + 2)
                        for k in range(KC):
                            qk(0, c, k)

                    for u in range(0, 4):
                        transpose_pair(u)
                        if u % 2:
                            first_qk(u // 2)
                            first_token(u // 2)
                    for u in range(4, 8):
                        transpose_pair(u)
                    first_qk(2)
                    first_qk(3)
                    first_token(2)
                    for k in range(STEPS):
                        for kind, n in events(k):
                            if kind == "FIRST":
                                first_token(n)
                            elif kind == "VALUES":
                                values(*n)
                            elif kind == "A":
                                n, h = n
                                g, t = divmod(n, NT)
                                if h == 0 and (t == 0 or t == 7):
                                    pe.wait_ge(stack_sem(g, int(t == 7)), stacked(g))
                                i = HG * n + h
                                if i >= len(a_ring):
                                    pe.wait_ge(S["a_free"], i - len(a_ring) + 1)
                                for s in range(4):
                                    q = P * t + SP * s
                                    last = pe.matmul(a_ring[i % len(a_ring)][SP * s:SP * (s + 1), 0:WIN],
                                                     q_stack[g % 2][0:KROWS, h, q:q + SP],
                                                     k_stack[g % 2][0:KROWS, h, q:q + WIN],
                                                     start=True, stop=True)
                                last.then_inc(S["a_full"], 1)
                            elif kind == "QK":
                                qk(*n)
                            elif kind == "MAX":
                                pe.wait_ge(S["max_ready"], n + 1)
                                misc_bank()
                                pe.transpose(misc[0:NT * HG, 0:P],
                                             row_max[:, n, :, :].rearrange("p h t -> p (h t)"), ident)\
                                  .then_inc(S["misc_full"], 1)
                            elif kind == "B":
                                n, h = n
                                g, j = divmod(n, NT)
                                c0, c1 = window(j)
                                if j == 0 and h == 0:
                                    pe.wait_ge(S["max_stacked"], MAX_STACKED * (g + 1))
                                i = HG * n + h
                                if i >= S_RING:
                                    pe.wait_ge(S["exp_ready"], i - S_RING + 1)
                                pe.matmul(s_banks[:, i % S_RING, c0:c1],
                                          k_stack[g % 2][:, h, WINDOW + P * j:WINDOW + P * (j + 1)],
                                          q_stack[g % 2][:, h, P * (j - 1) + c0:P * (j - 1) + c1],
                                          start=True, stop=True).then_inc(S["b_full"], 1)
                            elif kind == "PV":
                                n, part = n
                                g, i = divmod(n, NT)
                                j = i - 1 + part
                                pe.wait_ge(S["band_ready"], band_count(NT * g + j))
                                first, final = part == 0 or i == 0 and part == 1, part == 2 or j == NT - 1
                                if first and n % 4 == 0 and n:
                                    pe.wait_ge(S["o_copied"], n // 4)
                                for h in range(HG):
                                    head = HG * g + h
                                    last = pe.matmul(
                                        o_bank[SP * h:SP * (h + 1), P * (i % 4):P * (i % 4 + 1)],
                                        v_sb[:, j, VW * head:VW * head + SP],
                                        probs[:, j % 4, h, P * (i - j + 1):P * (i - j + 2)],
                                        start=first, stop=final)
                                last.then_inc(S["pv_done"], 1)
                            elif kind == "TURN":
                                pe.wait_ge(S["o_copied"], n + 1)
                                misc_bank()
                                for i in range(4):
                                    last = pe.transpose(misc[:, P * i:P * (i + 1)], o_raw[:, P * i:P * (i + 1)],
                                                        ident)
                                last.then_inc(S["misc_full"], 1)

                @block.scalar
                def _(act):
                    used = [0]

                    turned = [0]

                    def piece1(g, c):
                        used[0] += 1
                        if g >= 1:
                            act.wait_ge(stack_sem(g - 1, c // 2), stacked(g - 1))
                        act.wait_ge(S["misc_full"], used[0])
                        act.activation(piece[c // 2][:, 0, 512 * (c % 2):512 * (c % 2 + 1)], misc[:, :], ACT.Copy)\
                           .then_inc(S["piece1_ready"], 1)

                    def take_xnT(u):
                        act.wait_ge(S["xnT_psum"], u + 1)
                        act.activation(xnT[:, :, 2 * P * u:2 * P * (u + 1)],
                                       bank[u % 2][:, :].rearrange("p (k n) -> p k n", k=KC),
                                       ACT.Copy).then_inc(S["xnT_ready"], 1)

                    for u in range(8):
                        take_xnT(u)
                        if u == 1 or u == 3:
                            piece1(0, u // 2)
                    act.wait_ge(S["xn_ready"], NT)
                    piece1(0, 2)
                    piece1(0, 3)
                    act.wait_ge(S["pe_step"], 3)
                    act.activation(strip_rows, s_banks[:, 2, :], ACT.Copy).then_inc(S["act_step"], 1)
                    for k in range(STEPS):
                        for kind, n in events(k):
                            if kind == "VALUES" and n[1] == 3:
                                n = n[0]
                                act.wait_ge(S["v_psum"], n + 1)
                                act.activation(v_heads[:, 2 * n:2 * n + 2, :, 0:HD],
                                               s_banks[:, n % 2, :].rearrange("p (t h c) -> p t h c", t=2, c=HD),
                                               ACT.Copy).then_inc(S["v_ready"], 1)
                            elif kind == "FIRST" and n == 5:
                                act.wait_ge(S["dve_step"], NG + 6)
                                act.activation(pgT[:, :, 0:H], sg_arg, ACT.Exp, scale=LOGIT_SCALE)\
                                   .then_inc(S["act_step"], 1)
                            elif kind == "PIECE1":
                                piece1(*n)
                            elif kind == "MAX":
                                used[0] += 1
                                act.wait_ge(S["p0_arg_ready"], n + 1)
                                act.activation(p0[:, n, :, :], p0_arg[:, :, :], ACT.Exp,
                                               scale=LOGIT_SCALE).then_inc(S["p0_ready"], 1)
                            elif kind == "B":
                                n, h = n
                                g, j = divmod(n, NT)
                                c0, c1 = window(j)
                                if n >= 4 and h == 0:
                                    act.wait_ge(S["pv_done"], pv_count(n - 3, 0))
                                i = HG * n + h
                                act.wait_ge(S["b_full"], i + 1)
                                act.activation(probs[:, j % 4, h, c0:c1], s_banks[:, i % S_RING, c0:c1],
                                               ACT.Exp, scale=LOGIT_SCALE).then_inc(S["exp_ready"], 1)
                            elif kind == "COPY_OUT":
                                act.wait_ge(S["pv_done"], pv_count(4 * n + 3, 2))
                                if n:
                                    act.wait_ge(S["misc_full"], turned[0])
                                act.activation(o_raw[:, :], o_bank[:, :], ACT.Copy).then_inc(S["o_copied"], 1)
                            elif kind == "TURN":
                                used[0] += 1
                                turned[0] = used[0]

                @block.gpsimd
                def _(pool):
                    def piece3(g, c):
                        n = 4 * g + c
                        if g >= 1:
                            pool.wait_ge(stack_sem(g - 1, c // 2), stacked(g - 1))
                        pool.wait_ge(S["piece2_ready"], n + 1)
                        cols = slice(512 * (c % 2), 512 * (c % 2 + 1))
                        pool.tensor_tensor(piece[c // 2][:, SLOT_PIECE3, cols], rest[:, c % 2, :],
                                           piece[c // 2][:, SLOT_PIECE2, cols], ALU.subtract)\
                            .then_inc(S["piece3_ready"], 1)

                    def inverse_deviation(c):
                        pool.wait_ge(S["moments_ready"], 4 * c + 4)
                        pool.tensor_scalar(var_eps[:, 4 * c:4 * c + 4], mean_var[:, 4 * c:4 * c + 4, 1],
                                           EPS, None, ALU.add).then_inc(S["eps_added"], 1)
                        pool.wait_ge(S["eps_added"], c + 1)
                        pool.tensor_tensor(rstd[:, 4 * c:4 * c + 4], var_eps[:, 4 * c:4 * c + 4],
                                           neg_half[:, :], ALU.pow).then_inc(S["rstd_ready"], 1)

                    for c in range(3):
                        inverse_deviation(c)
                    piece3(0, 0)
                    inverse_deviation(3)
                    for c in range(1, 4):
                        piece3(0, c)
                    pool.memset(v_heads[:, :, :, HD], 1.0)
                    pool.memset(v_sb[:, :, H * VW:], 0.0)
                    pool.memset(pgT[:, :, H:SP], 0.0).then_inc(S["pool_step"], 1)
                    for k in range(STEPS):
                        for kind, n in events(k):
                            if kind == "SPLIT":
                                piece3(*n)
                            elif kind == "CUT":
                                g, j = divmod(n, NT)
                                pool.wait_ge(S["exp_ready"], HG * (n + 1))
                                if j > 0:
                                    part = probs[:, j % 4, :, 0:P]
                                    pool.affine_select(out=part, in_=part, compare_op=ALU.is_ge, fill=0.0,
                                                       base=0, pattern=[[0, HG], [1, P]],
                                                       channel_multiplier=-1).then_inc(S["band_ready"], 1)
                                if j < NT - 1:
                                    part = probs[:, j % 4, :, 2 * P:3 * P]
                                    pool.affine_select(out=part, in_=part, compare_op=ALU.is_ge, fill=0.0,
                                                       base=0, pattern=[[0, HG], [-1, P]],
                                                       channel_multiplier=1).then_inc(S["band_ready"], 1)
                            elif kind == "GLOB":
                                g, quartet = divmod(n, 4)
                                pool.wait_ge(S["p0_ready"], g + 1)
                                if n:
                                    pool.wait_ge(S["o_added"], n)
                                pool.tensor_tensor(
                                    glob_term[:, :, :, :],
                                    v0_all[:, VW * HG * g:VW * HG * (g + 1)]
                                    .rearrange("p (o h c) -> p o h c", o=1, c=VW).to_broadcast([P, 4, HG, VW]),
                                    p0[:, g, 4 * quartet:4 * quartet + 4, :].unsqueeze(3)
                                    .to_broadcast([P, 4, HG, VW]), ALU.mult).then_inc(S["glob_ready"], 1)

                @block.vector
                def _(dve):
                    used = [0]

                    def split(g, c):
                        n = 4 * g + c
                        used[0] += 1
                        half = piece[c // 2]
                        cols = slice(512 * (c % 2), 512 * (c % 2 + 1))
                        dve.wait_ge(S["piece1_ready"], n + 1)
                        if n >= 2:
                            dve.wait_ge(S["piece3_ready"], n - 1)
                        dve.tensor_tensor(rest[:, c % 2, :], misc[:, :], half[:, 0, cols], ALU.subtract)\
                           .then_inc(S["misc_free"], 1)
                        if g >= 1:
                            dve.wait_ge(stack_sem(g - 1, c // 2), stacked(g - 1))
                        dve.wait_ge(S["misc_free"], used[0])
                        dve.tensor_copy(half[:, SLOT_PIECE2, cols], rest[:, c % 2, :]).then_inc(S["piece2_ready"], 1)

                    def fill_slots(g, half, copies):
                        n = 2 * g + half
                        dve.wait_ge(S["piece2_ready"], 2 * n + 2)
                        for i in copies:
                            to, frm = ((1, 0), (4, 0), (6, 0), (3, SLOT_PIECE2))[i]
                            dve.tensor_copy(piece[half][:, to, :], piece[half][:, frm, :])\
                               .then_inc(S["slots_ready"], 1)

                    def moments(c):
                        dve.wait_ge(S[f"x_in{c}"], 16)
                        if c:
                            dve.wait_ge(S["moments_ready"], 4 * c)
                        for t in range(4 * c, 4 * c + 4):
                            dve.bn_stats(stats[:, t % 4, :], x_b[:, t, :]).then_inc(S["stats_ready"], 1)
                        for t in range(4 * c, 4 * c + 4):
                            dve.wait_ge(S["stats_ready"], t + 1)
                            dve.bn_aggr(mean_var[:, t, :], stats[:, t % 4, :]).then_inc(S["moments_ready"], 1)

                    def normalise(c):
                        dve.wait_ge(S["rstd_ready"], c + 1)
                        if c >= 2:
                            dve.wait_ge(S["xnT_psum"], 2 * c - 2)
                        for t in range(4 * c, 4 * c + 4):
                            dve.tensor_scalar(xn[:, t % 8, :], x_b[:, t, :], mean_var[:, t, 0:1],
                                              rstd[:, t:t + 1], ALU.subtract, ALU.mult)\
                               .then_inc(S["xn_ready"], 1)

                    def first_token(stage):
                        dve.wait_ge(S["pe_step"], stage + 1)
                        if stage == 0:
                            for g in range(NG):
                                dve.tensor_scalar(first_scaled[:, g, :], pick[:, g, :], o_bank[:, g:g + 1], None,
                                                  ALU.mult).then_inc(S["dve_step"], 1)
                        elif stage == 1:
                            dve.tensor_copy(uw[:, :, :], o_bank[:, 64:64 + KC * SP]
                                            .rearrange("p (k c) -> p k c", k=KC))\
                               .then_inc(S["dve_step"], 1)
                        elif stage == 2:
                            dve.wait_ge(S["act_step"], 1)
                            dve.tensor_reduce(small[:, 0:1], strip_rows, AX.X, ALU.max)\
                               .then_inc(S["dve_step"], 1)
                        elif stage == 3:
                            dve.tensor_copy(s0T[:, :, :].rearrange("p (g c) h -> p g c h", g=4),
                                            o_bank[:, :].rearrange("p (c g e) -> p g c e", c=4, g=4)
                                            [:, :, :, H:2 * H]).then_inc(S["dve_step"], 1)
                        elif stage == 4:
                            dve.tensor_reduce(small[0:1, 32:32 + SP],
                                              s_banks[0:1, 2, 128:256].rearrange("p (g e) -> p e g", g=4),
                                              AX.X, ALU.max).then_inc(S["dve_step"], 1)
                        elif stage == 5:
                            dve.tensor_copy(small[:, 8:8 + H], s_banks[:, 2, 256:256 + H])\
                               .then_inc(S["dve_step"], 1)
                            dve.wait_ge(S["dve_step"], NG + 5)
                            dve.tensor_tensor(sg_arg, o_bank[:, :].rearrange("p (m e) -> p m e", m=NT)[:, :, 0:H],
                                              small[:, 8:8 + H].unsqueeze(1).to_broadcast([P, NT, H]),
                                              ALU.subtract).then_inc(S["dve_step"], 1)
                        elif stage == 6:
                            dve.tensor_copy(v0_all[:, :], s_banks[:, 2, 0:H * VW])\
                               .then_inc(S["dve_step"], 1)
                        elif stage == 7:
                            dve.tensor_tensor(masked_o0, o_bank[:, 0:H * VW], diag, ALU.mult)\
                               .then_inc(S["dve_step"], 1)
                        elif stage == 8:
                            dve.tensor_copy(o0_row, s_banks[0:1, 2, 0:H * VW])\
                               .then_inc(S["dve_step"], 1)
                            dve.wait_ge(S["dve_step"], NG + 9)
                            heads = o0_row.rearrange("p (h c) -> p h c", c=VW)
                            dve.reciprocal(small[0:1, 48:48 + H], heads[:, :, HD])\
                               .then_inc(S["dve_step"], 1)
                            dve.wait_ge(S["dve_step"], NG + 10)
                            dve.tensor_tensor(o0_norm, heads[:, :, 0:HD],
                                              small[0:1, 48:48 + H].unsqueeze(2).to_broadcast([1, H, HD]),
                                              ALU.mult)

                    moments(0)
                    moments(1)
                    normalise(0)
                    moments(2)
                    normalise(1)
                    split(0, 0)
                    moments(3)
                    normalise(2)
                    first_token(0)
                    split(0, 1)
                    fill_slots(0, 0, range(4))
                    normalise(3)
                    first_token(1)
                    split(0, 2)
                    split(0, 3)
                    fill_slots(0, 1, range(4))
                    first_token(2)
                    for k in range(STEPS):
                        for kind, n in events(k):
                            if kind == "FIRST":
                                first_token(n)
                            elif kind == "KEY0":
                                dve.wait_ge(S["a_free"], NT * HG * (n + 1))
                                maxima = row_max[:, n, :, :].rearrange("p h t -> p t h")
                                dve.tensor_tensor(maxima, maxima, s0T[:, :, HG * n:HG * n + HG], ALU.max)\
                                   .then_inc(S["max_ready"], 1)
                            elif kind == "A":
                                n, h = n
                                g, t = divmod(n, NT)
                                mask = band[0 if t == 0 else 2 if t == NT - 1 else 1]
                                i = HG * n + h
                                dve.wait_ge(S["a_full"], i + 1)
                                dve.tensor_tensor_reduce(
                                    out=a_ring[i % len(a_ring)][:, 0:WIN], in0=a_ring[i % len(a_ring)][:, 0:WIN], in1=mask,
                                    scale=1.0, scalar=con[:, C_LOWEST:C_LOWEST + 1], op0=ALU.add,
                                    op1=ALU.max, accum_out=row_max[:, g, h, t:t + 1]).then_inc(S["a_free"], 1)
                            elif kind == "SPLIT":
                                split(*n)
                            elif kind == "SLOTS":
                                fill_slots(*n)
                            elif kind == "MAX":
                                used[0] += 1
                                if n:
                                    dve.wait_ge(S["max_stacked"], MAX_STACKED * n)
                                    dve.wait_ge(S["p0_ready"], n)
                                dve.wait_ge(S["misc_full"], used[0])
                                turned = misc[0:NT * HG, 0:P]
                                dve.tensor_scalar(neg_max[0][:, :], turned, -1.0, None, ALU.mult)\
                                   .then_inc(S["max_piece"], 1)
                                dve.wait_ge(S["max_ready"], n + 1)
                                dve.tensor_tensor(
                                    p0_arg[:, 1:NT, :], s0T[:, 1:NT, HG * n:HG * n + HG],
                                    row_max[:, n, :, 1:NT].rearrange("p h t -> p t h"), ALU.subtract)\
                                   .then_inc(S["p0_diff"], 1)
                                dve.memset(p0_arg[:, 0, :], MASKED)
                                dve.wait_ge(S["p0_diff"], n + 1)
                                dve.memset(p0_arg[0:1, 1, :], MASKED).then_inc(S["p0_arg_ready"], 1)
                                dve.wait_ge(S["max_piece"], 3 * n + 1)
                                dve.scalar_tensor_tensor(out=neg_rest[:, :], in0=turned, scalar=-1.0,
                                                         in1=neg_max[0][:, :], op0=ALU.mult, op1=ALU.subtract)\
                                   .then_inc(S["misc_free"], 1)
                                dve.wait_ge(S["misc_free"], used[0])
                                dve.tensor_copy(neg_max[1][:, :], neg_rest[:, :]).then_inc(S["max_piece"], 1)
                                dve.wait_ge(S["max_piece"], 3 * n + 2)
                                dve.tensor_tensor(neg_max[2][:, :], neg_rest[:, :], neg_max[1][:, :],
                                                  ALU.subtract).then_inc(S["max_piece"], 1)
                            elif kind == "OUT":
                                g, quartet = divmod(n, 4)
                                used[0] += 1
                                dve.wait_ge(S["misc_full"], used[0])
                                dve.wait_ge(S["glob_ready"], n + 1)
                                if n:
                                    dve.wait_ge(S["attn_ready"], n)
                                dve.tensor_tensor(
                                    o_add[:, :, :, :].rearrange("p t h c -> p (t h) c"),
                                    misc[:, :].rearrange("p (th c) -> p th c", c=SP)[:, :, 0:VW],
                                    glob_term[:, :, :, :].rearrange("p t h c -> p (t h) c"), ALU.add)\
                                   .then_inc(S["o_added"], 1)
                                dve.wait_ge(S["o_added"], n + 1)
                                dve.reciprocal(recip[:, :, :], o_add[:, :, :, HD]).then_inc(S["misc_free"], 1)
                                dve.wait_ge(S["misc_free"], used[0])
                                dve.tensor_tensor(
                                    attn[:, 4 * quartet:4 * quartet + 4, HG * HD * g:HG * HD * (g + 1)]
                                    .rearrange("p t (h c) -> p t h c", c=HD),
                                    o_add[:, :, :, 0:HD],
                                    recip[:, :, :].unsqueeze(3).to_broadcast([P, 4, HG, HD]), ALU.mult)\
                                   .then_inc(S["attn_ready"], 1)
                    dve.wait_ge(S["attn_ready"], A_STEPS // 4)
                    dve.tensor_copy(attn[0:1, 0, :], o0_norm.rearrange("p h c -> p (h c)"))
            reset()

        with nc.Fori(0, B) as b:
            norm_block(NT, load=load_batch(x, b), gate_to=lambda: logits[:, bass.ds(b * NT, NT), :])
        first_any = route()
        with nc.If(first_any != 0):
            experts(x, x1)

        with nc.Fori(0, B) as b:
            def load(sp):
                with sp.If(first_any != 0):
                    load_batch(x1, b)(sp)
                with sp.Else():
                    load_batch(x, b)(sp)
            attention_block(load)
            norm_block(NT, load=load, gate_to=lambda: logits[:, bass.ds(b * NT, NT), :], project=True,
                       store=lambda c: out[bass.ds(b, 1), 512 * c:512 * (c + 1), :]
                       .rearrange("o (t p) d -> p (o t) d", p=P))
        second_any = route()
        with nc.If(second_any != 0):
            experts(out, out)


def constants():
    import numpy as np
    con = np.zeros((P, C_END), np.float32)
    con[:, C_IDENT:C_IDENT + P] = np.eye(P)
    r = np.arange(P)[:, None] % SP
    strip = np.arange(P)[:, None] // SP
    c = np.arange(WIN)[None, :]
    outside = (c < r) | (c > 2 * WINDOW + r)
    key_first = SP * strip - WINDOW + c
    key_last = P * (NT - 1) + key_first
    for i, bad in enumerate((outside | (key_first < 0), outside, outside | (key_last >= T))):
        con[:, C_BAND + i * WIN:C_BAND + (i + 1) * WIN] = np.where(bad, MASKED, 0.0)
    pick = con[:, C_PICK:C_PICK + NG * SP].reshape(P, NG, SP)
    pick = np.zeros((P, NG, SP), np.float32)
    for p in range(P):
        for g in range(NG):
            half, row = divmod(p, HG * HD)
            pick[p, g, H * half + HG * g + row // HD] = 1.0
    con[:, C_PICK:C_PICK + NG * SP] = pick.reshape(P, -1)
    diag = np.zeros((P, H, VW), np.float32)
    for p in range(P):
        if p % SP < H:
            diag[p, p % SP, :] = 1.0
    con[:, C_DIAG:C_DIAG + H * VW] = diag.reshape(P, -1)
    con[:, C_RANK:C_RANK + E] = E - np.arange(E)
    con[:, C_LOWEST] = MASKED
    return con


def chunked(w):
    return w.reshape(w.shape[0] // P, P, w.shape[1]).transpose(1, 0, 2)


def kernel(**inputs):
    import numpy as np
    import concourse.bacc as bacc
    from concourse.bass_utils import run_bass_kernel_spmd

    a = {k.replace("L0_", ""): np.asarray(v) for k, v in inputs.items()}
    wq, wk = a["attn_Wq"], a["attn_Wk"]
    n = HG * HD
    wqk = np.stack([np.concatenate([chunked(wq.T)[:, :, g * n:(g + 1) * n], chunked(wk.T)[:, :, g * n:(g + 1) * n]],
                                   axis=2) for g in range(NG)], axis=1)
    wback = np.stack([np.concatenate([wk[g * n:(g + 1) * n], wq[g * n:(g + 1) * n]], axis=0)
                      for g in range(NG)], axis=1)
    laid = {
        "x": a["attn_x"], "wqk": wqk, "wback": wback, "wv": chunked(a["attn_Wv"].T), "wo": chunked(a["attn_Wo"].T),
        "gate": chunked(a["ffn_gate_w"].T),
        "w1": np.stack([chunked(a["ffn_w1"][e].T) for e in range(E)]),
        "b1": a["ffn_b1"].reshape(E, KC, P).transpose(0, 2, 1),
        "w2": np.stack([chunked(a["ffn_w2"][e].T) for e in range(E)]),
        "b2": a["ffn_b2"], "consts": constants(),
    }
    nc = bacc.Bacc("TRN2", target_bir_lowering=False, num_devices=1)
    arrays, args = {}, {}
    for name, array in laid.items():
        arrays[f"in_{name}"] = np.ascontiguousarray(array)
        args[name] = nc.dram_tensor(f"in_{name}", array.shape, FP32, kind="ExternalInput").ap()
    x1 = nc.dram_tensor("x1_scratch", (B, T, D), FP32, kind="Internal").ap()
    out = nc.dram_tensor("out_x", (B, T, D), FP32, kind="ExternalOutput").ap()
    build(nc, x1=x1, out=out, **args)
    r = run_bass_kernel_spmd(nc, [arrays], core_ids=[0])
    return r.results[0]["out_x"]
```

```python
import concourse.bass as bass
from concourse import mybir
from contextlib import ExitStack

FP32 = mybir.dt.float32
BF16 = mybir.dt.bfloat16
I32 = mybir.dt.int32
ALU = mybir.AluOpType
ACT = mybir.ActivationFunctionType
AX = mybir.AxisListType

B, T, D = 4, 2048, 256
H, HD = 16, 16
E = 8
N = B * T
CAPACITY = int(1.25 * N / E)
EPS = 1e-5
LOGIT_SCALE = 0.25
WINDOW = 128

P = 128
NT = T // P
KC = D // P
HG = 4
NG = H // HG
SP = 32
VW = HD + 1
WIN = 2 * WINDOW + SP
TERMS = 6
SLOTS = TERMS + 1
SLOT_PIECE2, SLOT_PIECE3 = 2, 5
KROWS = HD * TERMS
SROWS = KROWS + 3
HALF = T // 2
MASKED = -1.0e30

C_IDENT = 0
C_BAND = C_IDENT + P
C_PICK = C_BAND + 3 * WIN
C_DIAG = C_PICK + NG * SP
C_RANK = C_DIAG + H * VW
C_LOWEST = C_RANK + E
C_END = C_LOWEST + 1


def build(nc, x, wqk, wback, wv, wo, gate, w1, b1, w2, b2, consts, x1, out):
    ctx = ExitStack()
    with ctx:
        def sb(name, shape, dt=FP32):
            return ctx.enter_context(nc.sbuf_tensor(name, shape, dt))

        q_stack = [sb(f"q_stack{i}", [P, HG, T], BF16) for i in range(2)]
        k_stack = [sb(f"k_stack{i}", [P, HG, T + 2 * WINDOW], BF16) for i in range(2)]
        xnT = sb("xnT", [P, KC, T])
        v_sb = sb("v_sb", [P, NT, H * VW + SP - VW])
        probs = sb("probs", [P, 4, HG, 3 * P])
        attn = sb("attn", [P, NT, D])
        x_b = sb("x_b", [P, NT, D])
        piece0 = sb("piece0", [P, SLOTS, HALF], BF16)
        rest = sb("rest", [P, 2, 512])
        wqk_sb = sb("wqk_sb", [P, NG, KC, P])
        wback_sb = sb("wback_sb", [P, NG, D])
        wv_sb = sb("wv_sb", [P, KC, D])
        wo_sb = sb("wo_sb", [P, KC, D])
        gate_sb = sb("gate_sb", [P, KC, SP])
        con = sb("con", [P, C_END])
        ones = sb("ones", [P, P])
        neg_half = sb("neg_half", [P, 4])
        v0_all = sb("v0_all", [P, H * VW])
        o_raw = sb("o_raw", [P, 4 * P])
        o_add = sb("o_add", [P, 4, HG, VW])
        glob_term = sb("glob_term", [P, 4, HG, VW])
        recip = sb("recip", [P, 4, HG])
        s0T = sb("s0T", [P, NT, H])
        row_max = sb("row_max", [P, NG, HG, NT])
        p0_arg = sb("p0_arg", [P, NT, HG])
        p0 = sb("p0", [P, NG, NT, HG])
        neg_max = [sb(f"neg_max{i}", [NT * HG, P], BF16) for i in range(3)]
        neg_rest = sb("neg_rest", [NT * HG, P])
        logits = sb("logits", [P, B * NT, E])
        stats = sb("stats", [P, 4, 6])
        mean_var = sb("mean_var", [P, NT, 2])
        var_eps = sb("var_eps", [P, NT])
        rstd = sb("rstd", [P, NT])
        small = sb("small", [P, 64])
        flags = sb("flags", [1, E + 1], I32)

        probs_flat = probs[:, :, :, :].rearrange("p a h n -> p (a h n)")
        attn_flat = attn[:, :, :].rearrange("p t d -> p (t d)")
        piece = [piece0[:, :, :], x_b[:, :, :].rearrange("p t d -> p (t d)").bitcast(BF16)
                 [:, 0:SLOTS * HALF].rearrange("p (s n) -> p s n", s=SLOTS)]
        o0_norm = x_b[0:1, NT - 1, :].rearrange("p (h c) -> p h c", c=HD)
        xn = probs_flat[:, 0:8 * D].rearrange("p (t d) -> p t d", t=8)
        piece0_flat = piece0[:, :, :].rearrange("p s n -> p (s n)").bitcast(FP32)
        xn_late = piece0_flat[:, 0:8 * D].rearrange("p (t d) -> p t d", t=8)
        attnT = piece0_flat[:, 8 * D:8 * D + 2 * 512].rearrange("p (s k n) -> p s k n", s=2, k=KC)
        strip_rows = probs_flat[:, 3072:3584]
        sg_arg = probs_flat[:, 3584:3840].rearrange("p (m h) -> p m h", h=H)
        masked_o0 = probs_flat[:, 3840:3840 + H * VW]
        o0_row = probs_flat[0:1, 4112:4112 + H * VW]
        pgT = probs_flat[:, 4400:4400 + NT * SP].rearrange("p (m c) -> p m c", c=SP)
        uw = probs_flat[:, 4912:4912 + KC * SP].rearrange("p (k c) -> p k c", k=KC)
        first_scaled = probs_flat[:, 4976:4976 + NG * SP].rearrange("p (g c) -> p g c", g=NG)
        wts = rest[:, 0, :].rearrange("p (t e) -> p t e", e=E)
        ident = con[:, C_IDENT:C_IDENT + P]
        band = [con[:, C_BAND + i * WIN:C_BAND + (i + 1) * WIN] for i in range(3)]
        pick = con[:, C_PICK:C_PICK + NG * SP].rearrange("p (g c) -> p g c", g=NG)
        diag = con[:, C_DIAG:C_DIAG + H * VW]
        rank = con[:, C_RANK:C_RANK + E]
        v_heads = v_sb[:, :, 0:H * VW].rearrange("p t (h c) -> p t h c", c=VW)

        bank = [ctx.enter_context(nc.psum_tensor(f"bank{i}", [P, 512], FP32)) for i in range(2)]
        s_banks = ctx.enter_context(nc.psum_tensor("s_banks", [P, 4, 512], FP32))
        o_bank = ctx.enter_context(nc.psum_tensor("o_bank", [P, 512], FP32))
        misc = ctx.enter_context(nc.psum_tensor("misc", [P, 512], FP32))
        attn_banks = [bank[0][:, :]] * 7 + [s_banks[:, 0, :]]
        project_banks = [bank[1][:, :]] * 7 + [s_banks[:, 1, :]]
        a_ring = [bank[0], bank[1], s_banks[:, 3, :]]
        S_RING = 3

        names = [f"x_in{c}" for c in range(8)] + ["consts_in", "stats_ready", "moments_ready",
                 "eps_added", "rstd_ready", "xn_ready", "xnT_psum", "xnT_ready", "v_psum", "v_ready",
                 "gate_psum", "gate_rows", "gate_cols", "logits_ready",
                 "proj_in_psum", "proj_in_sbuf", "proj_psum", "x2_ready", "stored", "first_row",
                 "pe_step", "dve_step", "act_step", "pool_step",
                 "misc_full", "misc_free", "piece1_ready", "piece2_ready", "piece3_ready", "slots_ready",
                 "stack00", "stack01", "stack10", "stack11", "a_full", "a_free",
                 "max_piece", "max_stacked", "max_ready", "p0_diff", "p0_arg_ready", "p0_ready",
                 "b_full", "exp_ready", "band_ready", "pv_done", "o_copied", "glob_ready", "o_added",
                 "attn_ready"]
        sems = {n: ctx.enter_context(nc.semaphore(n)) for n in names}
        nums = [s.num for s in sems.values()]
        assert max(nums) - min(nums) + 1 == len(nums)
        S = sems

        def reset():
            nc.all_engine_barrier(sems_to_clear=range(min(nums), max(nums) + 1))

        with nc.Block() as block:
            @block.sync
            def _(sp):
                for dst, src in ((con[:, :], consts), (wqk_sb[:, :, :, :], wqk), (wback_sb[:, :, :], wback),
                                 (wv_sb[:, :, :], wv), (wo_sb[:, :, :], wo), (gate_sb[:, :, 0:E], gate)):
                    sp.dma_start(dst, src).then_inc(S["consts_in"], 16)
                sp.wait_ge(S["consts_in"], 6 * 16)

            @block.vector
            def _(dve):
                dve.memset(ones[:, :], 1.0)
                dve.memset(neg_half[:, :], -0.5)
                dve.memset(gate_sb[:, :, E:SP], 0.0)
                for s in range(2):
                    dve.memset(k_stack[s][0:KROWS, :, 0:WINDOW], 0.0)
                    dve.memset(k_stack[s][0:KROWS, :, WINDOW + T:], 0.0)
                dve.memset(k_stack[1][KROWS:SROWS, :, :], 1.0)

            @block.gpsimd
            def _(pool):
                pool.memset(k_stack[0][KROWS:SROWS, :, :], 1.0)
        reset()

        def norm_block(ntiles, load):
            chunks = ntiles // 4
            pairs = ntiles // 2
            with nc.Block() as block:
                @block.sync
                def _(sp):
                    load(sp)

                @block.vector
                def _(dve):
                    def normalise(c):
                        dve.wait_ge(S["rstd_ready"], c + 1)
                        if c >= 2:
                            dve.wait_ge(S["xnT_psum"], 2 * c - 2)
                        for t in range(4 * c, 4 * c + 4):
                            dve.tensor_scalar(xn[:, t % 8, :], x_b[:, t, :], mean_var[:, t, 0:1],
                                              rstd[:, t:t + 1], ALU.subtract, ALU.mult)\
                               .then_inc(S["xn_ready"], 1)

                    for c in range(chunks):
                        dve.wait_ge(S[f"x_in{c}"], 16)
                        if c:
                            dve.wait_ge(S["moments_ready"], 4 * c)
                        for t in range(4 * c, 4 * c + 4):
                            dve.bn_stats(stats[:, t % 4, :], x_b[:, t, :]).then_inc(S["stats_ready"], 1)
                        for t in range(4 * c, 4 * c + 4):
                            dve.wait_ge(S["stats_ready"], t + 1)
                            dve.bn_aggr(mean_var[:, t, :], stats[:, t % 4, :]).then_inc(S["moments_ready"], 1)
                        if c >= 1:
                            normalise(c - 1)
                    normalise(chunks - 1)

                @block.gpsimd
                def _(pool):
                    for c in range(chunks):
                        pool.wait_ge(S["moments_ready"], 4 * c + 4)
                        pool.tensor_scalar(var_eps[:, 4 * c:4 * c + 4], mean_var[:, 4 * c:4 * c + 4, 1],
                                           EPS, None, ALU.add).then_inc(S["eps_added"], 1)
                        pool.wait_ge(S["eps_added"], c + 1)
                        pool.tensor_tensor(rstd[:, 4 * c:4 * c + 4], var_eps[:, 4 * c:4 * c + 4],
                                           neg_half[:, :], ALU.pow).then_inc(S["rstd_ready"], 1)

                @block.scalar
                def _(act):
                    def take_xnT(u):
                        act.wait_ge(S["xnT_psum"], u + 1)
                        act.activation(xnT[:, :, 2 * P * u:2 * P * (u + 1)],
                                       bank[u % 2][:, :].rearrange("p (k n) -> p k n", k=KC),
                                       ACT.Copy).then_inc(S["xnT_ready"], 1)

                    for u in range(pairs):
                        take_xnT(u)

                @block.tensor
                def _(pe):
                    def transpose_pair(u):
                        pe.wait_ge(S["xn_ready"], 2 * u + 2)
                        if u >= 2:
                            pe.wait_ge(S["xnT_ready"], u - 1)
                        for k in range(KC):
                            for i in range(2):
                                last = pe.transpose(bank[u % 2][:, k * 2 * P + i * P:k * 2 * P + (i + 1) * P],
                                                    xn[:, (2 * u + i) % 8, k * P:(k + 1) * P], ident)
                        last.then_inc(S["xnT_psum"], 1)

                    for u in range(pairs):
                        transpose_pair(u)
            reset()

        def load_batch(dram, b):
            def load(sp, chunks=range(NT // 4)):
                for c in chunks:
                    sp.dma_start(x_b[:, 4 * c:4 * c + 4, :],
                                 dram[bass.ds(b, 1), 512 * c:512 * (c + 1), :]
                                 .rearrange("o (t p) d -> p (o t) d", p=P)).then_inc(S[f"x_in{c}"], 16)
            return load

        def first_logits_block(i):
            chunks, pairs = 2 * NT // 4, NT

            def x_tile(t):
                return x_b[:, t, :] if t < NT else attn[:, t - NT, :]

            with nc.Block() as block:
                @block.sync
                def _(sp):
                    for c in range(chunks):
                        to = x_b if c < 4 else attn
                        sp.dma_start(to[:, 4 * (c % 4):4 * (c % 4) + 4, :],
                                     x[bass.ds(2 * i + c // 4, 1), 512 * (c % 4):512 * (c % 4 + 1), :]
                                     .rearrange("o (t p) d -> p (o t) d", p=P)).then_inc(S[f"x_in{c}"], 16)

                @block.vector
                def _(dve):
                    def moments(c):
                        dve.wait_ge(S[f"x_in{c}"], 16)
                        if c:
                            dve.wait_ge(S["moments_ready"], 4 * c)
                        for t in range(4 * c, 4 * c + 4):
                            dve.bn_stats(stats[:, t % 4, :], x_tile(t)).then_inc(S["stats_ready"], 1)
                        for t in range(4 * c, 4 * c + 4):
                            dve.wait_ge(S["stats_ready"], t + 1)
                            dve.bn_aggr(mean_var[:, t % NT, :], stats[:, t % 4, :])\
                               .then_inc(S["moments_ready"], 1)

                    def normalise(c):
                        dve.wait_ge(S["rstd_ready"], c + 1)
                        if c >= 2:
                            dve.wait_ge(S["xnT_psum"], 2 * c - 2)
                        for t in range(4 * c, 4 * c + 4):
                            dve.tensor_scalar(xn[:, t % 8, :], x_tile(t), mean_var[:, t % NT, 0:1],
                                              rstd[:, t % NT:t % NT + 1], ALU.subtract, ALU.mult)\
                               .then_inc(S["xn_ready"], 1)

                    def take_logits(half):
                        dve.wait_ge(S["gate_cols"], half + 1)
                        dve.tensor_copy(
                            logits[:, bass.ds((2 * i + half) * NT, NT), :].rearrange("p (g c) e -> p g c e", g=4),
                            s_banks[:, 3, :].rearrange("p (c g e) -> p g c e", c=4, g=4)[:, :, :, 0:E])\
                           .then_inc(S["logits_ready"], 1)

                    for c in range(chunks):
                        moments(c)
                        if c >= 1:
                            normalise(c - 1)
                        if c == chunks - 1:
                            take_logits(0)
                    normalise(chunks - 1)
                    take_logits(1)

                @block.gpsimd
                def _(pool):
                    for c in range(chunks):
                        at = slice(4 * (c % 4), 4 * (c % 4) + 4)
                        pool.wait_ge(S["moments_ready"], 4 * c + 4)
                        pool.tensor_scalar(var_eps[:, at], mean_var[:, at, 1], EPS, None, ALU.add)\
                            .then_inc(S["eps_added"], 1)
                        pool.wait_ge(S["eps_added"], c + 1)
                        pool.tensor_tensor(rstd[:, at], var_eps[:, at], neg_half[:, :], ALU.pow)\
                            .then_inc(S["rstd_ready"], 1)

                @block.scalar
                def _(act):
                    for u in range(pairs):
                        cols = slice(2 * P * (u % 8), 2 * P * (u % 8 + 1))
                        act.wait_ge(S["xnT_psum"], u + 1)
                        if u == 8:
                            act.wait_ge(S["gate_psum"], 1)
                            act.activation(strip_rows, misc[:, :], ACT.Copy).then_inc(S["gate_rows"], 1)
                        act.activation(xnT[:, :, cols], bank[u % 2][:, :].rearrange("p (k n) -> p k n", k=KC),
                                       ACT.Copy).then_inc(S["xnT_ready"], 1)
                    act.wait_ge(S["gate_psum"], 2)
                    act.wait_ge(S["gate_cols"], 1)
                    act.activation(strip_rows, misc[:, :], ACT.Copy).then_inc(S["gate_rows"], 1)

                @block.tensor
                def _(pe):
                    def transpose_pair(u):
                        pe.wait_ge(S["xn_ready"], 2 * u + 2)
                        if u >= 2:
                            pe.wait_ge(S["xnT_ready"], u - 1)
                        for k in range(KC):
                            for t in range(2):
                                last = pe.transpose(bank[u % 2][:, k * 2 * P + t * P:k * 2 * P + (t + 1) * P],
                                                    xn[:, (2 * u + t) % 8, k * P:(k + 1) * P], ident)
                        last.then_inc(S["xnT_psum"], 1)

                    def gate_products(half):
                        pe.wait_ge(S["xnT_ready"], 8 * (half + 1))
                        if half:
                            pe.wait_ge(S["gate_rows"], 1)
                        for k in range(KC):
                            for g in range(4):
                                last = pe.matmul(misc[SP * g:SP * (g + 1), :], gate_sb[:, k, :],
                                                 xnT[:, k, 512 * g:512 * (g + 1)],
                                                 start=(k == 0), stop=(k == KC - 1))
                        last.then_inc(S["gate_psum"], 1)

                    def turn_logits(half):
                        pe.wait_ge(S["gate_rows"], half + 1)
                        if half:
                            pe.wait_ge(S["logits_ready"], 1)
                        for c in range(4):
                            last = pe.transpose(s_banks[:, 3, P * c:P * (c + 1)],
                                                strip_rows[:, P * c:P * (c + 1)], ident)
                        last.then_inc(S["gate_cols"], 1)

                    for u in range(pairs):
                        transpose_pair(u)
                        if u == 7:
                            gate_products(0)
                        elif u == 9:
                            turn_logits(0)
                    gate_products(1)
                    turn_logits(1)
            reset()

        def route():
            L = B * NT
            tmp = [attn_flat[:, i * 512:(i + 1) * 512].rearrange("p (t e) -> p t e", e=E) for i in range(6)]
            row = [attn_flat[:, 3072 + i * L:3072 + (i + 1) * L] for i in range(4)]
            counts = attn_flat[:, 3600:3600 + E]
            keep = attn_flat[:, 3616:3616 + E + 1]

            def wide(r):
                return r.unsqueeze(2).to_broadcast([P, L, E])

            rank_all = rank.unsqueeze(1).to_broadcast([P, L, E])
            with nc.Block() as block:
                @block.vector
                def _(dve):
                    done = [0]

                    def step(ins):
                        done[0] += 1
                        ins.then_inc(S["dve_step"], 1)
                        dve.wait_ge(S["dve_step"], done[0])

                    step(dve.tensor_reduce(row[0], logits[:, :, :], AX.X, ALU.max))
                    step(dve.tensor_tensor(tmp[0], logits[:, :, :], wide(row[0]), ALU.subtract))
                    dve.wait_ge(S["act_step"], 1)
                    step(dve.tensor_reduce(row[1], tmp[1], AX.X, ALU.add))
                    step(dve.reciprocal(row[2], row[1]))
                    probs_e = tmp[0]
                    step(dve.tensor_tensor(probs_e, tmp[1], wide(row[2]), ALU.mult))

                    def pick_first_largest(values, selected, a):
                        step(dve.tensor_reduce(row[0], values, AX.X, ALU.max))
                        step(dve.tensor_tensor(a, values, wide(row[0]), ALU.is_equal))
                        step(dve.tensor_tensor(a, a, rank_all, ALU.mult))
                        step(dve.tensor_reduce(row[1], a, AX.X, ALU.max))
                        step(dve.tensor_tensor(selected, rank_all, wide(row[1]), ALU.is_equal))

                    pick_first_largest(probs_e, tmp[2], tmp[1])
                    step(dve.scalar_tensor_tensor(out=tmp[3], in0=tmp[2], scalar=-4.0, in1=probs_e,
                                                  op0=ALU.mult, op1=ALU.add))
                    pick_first_largest(tmp[3], tmp[4], tmp[1])
                    step(dve.tensor_tensor(tmp[2], tmp[2], tmp[4], ALU.add))
                    step(dve.tensor_reduce(counts, tmp[2].rearrange("p t e -> p e t"), AX.X, ALU.add))
                    dve.wait_ge(S["pe_step"], 1)
                    step(dve.tensor_scalar(keep[:, 0:E], misc[:, 0:E], float(CAPACITY), None, ALU.is_le))
                    step(dve.tensor_reduce(keep[:, E:E + 1], keep[:, 0:E], AX.X, ALU.max))
                    step(dve.tensor_copy(flags[0:1, :], keep[0:1, :]))
                    step(dve.tensor_tensor(tmp[3], tmp[2], probs_e, ALU.mult))
                    step(dve.scalar_tensor_tensor(out=wts[:, :, :], in0=tmp[3], scalar=0.5,
                                                  in1=keep[:, 0:E].unsqueeze(1).to_broadcast([P, L, E]),
                                                  op0=ALU.mult, op1=ALU.mult))

                @block.scalar
                def _(act):
                    act.wait_ge(S["dve_step"], 2)
                    act.activation(tmp[1], tmp[0], ACT.Exp).then_inc(S["act_step"], 1)

                @block.tensor
                def _(pe):
                    pe.wait_ge(S["dve_step"], 18)
                    pe.matmul(misc[:, 0:E], ones[:, :], counts, start=True, stop=True)\
                      .then_inc(S["pe_step"], 1)
            reset()
            return nc.values_load(flags[0:1, E:E + 1], min_val=0, max_val=1)

        def experts(src, dst):
            pool_w = v_sb[:, :, :].rearrange("p t c -> p (t c)")
            w1_sb = pool_w[:, 0:KC * D].rearrange("p (k n) -> p k n", k=KC)
            w2_sb = pool_w[:, 512:512 + KC * D].rearrange("p (k n) -> p k n", k=KC)
            b1_sb = pool_w[:, 1024:1024 + KC]
            b2_sb = pool_w[0:1, 1280:1280 + D]
            hT = pool_w[:, 1536:1536 + KC * 512].rearrange("p (k n) -> p k n", k=KC)
            weight = pool_w[:, 2600:2604]

            def chunk_of(dram, c):
                return dram.rearrange("b t d -> (b t) d").rearrange("(c t p) d -> c p t d", t=4, p=P)[
                    bass.ds(c, 1)].rearrange("o p t d -> p (o t) d")

            with nc.Fori(0, N // 512) as c:
                norm_block(4, load=lambda sp: sp.dma_start(x_b[:, 0:4, :], chunk_of(src, c))
                           .then_inc(S["x_in0"], 16))
                with nc.Fori(0, E) as e:
                    kept = nc.values_load(flags[0:1, bass.ds(e, 1)], min_val=0, max_val=1)
                    with nc.If(kept != 0):
                        with nc.Block() as block:
                            @block.sync
                            def _(sp):
                                for to, frm in ((w1_sb, w1[bass.ds(e, 1)].rearrange("o p k n -> p (o k) n")),
                                                (w2_sb, w2[bass.ds(e, 1)].rearrange("o p k n -> p (o k) n")),
                                                (b1_sb, b1[bass.ds(e, 1)].rearrange("o p k -> p (o k)")),
                                                (b2_sb, b2[bass.ds(e, 1), :])):
                                    sp.dma_start(to, frm).then_inc(S["consts_in"], 16)

                            @block.tensor
                            def _(pe):
                                pe.wait_ge(S["consts_in"], 64)
                                for f in range(KC):
                                    for k in range(KC):
                                        last = pe.matmul(bank[f][:, :], w1_sb[:, k, f * P:(f + 1) * P],
                                                         xnT[:, k, 0:512], start=(k == 0), stop=(k == KC - 1))
                                    last.then_inc(S["pe_step"], 1)
                                pe.wait_ge(S["act_step"], 2 * KC)
                                for t in range(4):
                                    o = s_banks[:, t, 0:D]
                                    for k in range(KC):
                                        pe.matmul(o, hT[:, k, t * P:(t + 1) * P], w2_sb[:, k, :],
                                                  start=(k == 0), stop=False)
                                    pe.matmul(o, ones[0:1, :], b2_sb, start=False, stop=True)\
                                      .then_inc(S["pe_step"], 1)

                            @block.scalar
                            def _(act):
                                act.wait_ge(S["consts_in"], 64)
                                for f in range(KC):
                                    act.wait_ge(S["pe_step"], f + 1)
                                    act.activation(hT[:, f, :], bank[f][:, :], ACT.Silu,
                                                   bias=b1_sb[:, f:f + 1]).then_inc(S["act_step"], 2)

                            @block.gpsimd
                            def _(pool):
                                pool.tensor_copy(weight, wts[:, bass.ds(c * 4, 4), bass.ds(e, 1)]
                                                 .rearrange("p t o -> p (t o)")).then_inc(S["pool_step"], 1)

                            @block.vector
                            def _(dve):
                                dve.wait_ge(S["pool_step"], 1)
                                for t in range(4):
                                    dve.wait_ge(S["pe_step"], KC + t + 1)
                                    dve.scalar_tensor_tensor(out=x_b[:, t, :], in0=s_banks[:, t, 0:D],
                                                             scalar=weight[:, t:t + 1], in1=x_b[:, t, :],
                                                             op0=ALU.mult, op1=ALU.add)
                        reset()
                with nc.Block() as block:
                    @block.sync
                    def _(sp):
                        sp.dma_start(chunk_of(dst, c), x_b[:, 0:4, :]).then_inc(S["stored"], 16)
                        sp.wait_ge(S["stored"], 16)
                reset()

        EARLY_CHUNKS, EARLY_NORMALISED = 3, 2

        def moments(dve, c, done):
            if done:
                dve.wait_ge(S["moments_ready"], done)
            for t in range(4):
                dve.bn_stats(stats[:, t, :], x_b[:, 4 * c + t, :]).then_inc(S["stats_ready"], 1)
            for t in range(4):
                dve.wait_ge(S["stats_ready"], done + t + 1)
                dve.bn_aggr(mean_var[:, 4 * c + t, :], stats[:, t, :]).then_inc(S["moments_ready"], 1)

        def inverse_deviation(pool, c, n):
            tiles = slice(4 * c, 4 * c + 4)
            pool.wait_ge(S["moments_ready"], 4 * n + 4)
            pool.tensor_scalar(var_eps[:, tiles], mean_var[:, tiles, 1], EPS, None, ALU.add)\
                .then_inc(S["eps_added"], 1)
            pool.wait_ge(S["eps_added"], n + 1)
            pool.tensor_tensor(rstd[:, tiles], var_eps[:, tiles], neg_half[:, :], ALU.pow)\
                .then_inc(S["rstd_ready"], 1)

        def normalise(dve, c, ring):
            for t in range(4 * c, 4 * c + 4):
                dve.tensor_scalar(ring[:, t % 8, :], x_b[:, t, :], mean_var[:, t, 0:1],
                                  rstd[:, t:t + 1], ALU.subtract, ALU.mult).then_inc(S["xn_ready"], 1)

        def early_moments(dve, loads, n):
            for c in range(EARLY_CHUNKS):
                dve.wait_ge(S[f"x_in{c}"], 16 * loads)
                moments(dve, c, 4 * (n + c))
                if 1 <= c <= EARLY_NORMALISED:
                    dve.wait_ge(S["rstd_ready"], n + c)
                    normalise(dve, c - 1, xn)

        LATE_CHUNKS = 4 - EARLY_CHUNKS
        LATE_TILES = NT - 4 * EARLY_NORMALISED

        A_STEPS = NG * NT
        LAG_B, LAG_PV, LAG_OUT = NT + 3, NT + 6, NT + 7
        PROJECT_FROM = A_STEPS + LAG_OUT - NT + 4
        STEPS = PROJECT_FROM + 4 * 3 + 6
        QK_AT = {3: 0, 7: 1, 11: 2, 15: 3}
        FIRST_AT = (1, 2, 3, 5, 6, 9, 17, 18)
        SLOTS_AT = {9: (0, (0, 1)), 10: (0, (2, 3)), 17: (1, (0, 1)), 18: (1, (2, 3))}

        PROJECT_STAGES = {0: ("TURN_ATTN", 0), 3: ("PROJECT", 0), 5: ("TURN_ATTN", 1), 8: ("PROJECT", 1),
                          10: ("MOMENTS", 0), 15: ("NORMALISE", 0), 17: ("TURN_XN", 0), 19: ("TURN_XN", 1)}
        LAST_STAGES = {0: ("TURN_ATTN", 0), 1: ("TURN_ATTN", 1), 4: ("PROJECT", 0), 5: ("PROJECT", 1),
                       10: ("MOMENTS", 0), 15: ("NORMALISE", 0), 17: ("TURN_XN", 0), 19: ("TURN_XN", 1),
                       20: ("NEXT", 0), 22: ("LOGITS", 0)}

        def band_count(n):
            g, j = divmod(n, NT)
            return g * (2 * NT - 2) + min(1 + 2 * j, 2 * NT - 2)

        def pv_count(n, part):
            g, i = divmod(n, NT)
            return g * (3 * NT - 2) + min(3 * i + part, 3 * NT - 2)

        def next_groups(k, at):
            return [g for g in range(1, NG) if k - NT * (g - 1) == at]

        def products_with_v(k, parts):
            if 0 <= k - LAG_PV < A_STEPS:
                for part in parts:
                    if 0 <= (k - LAG_PV) % NT + part - 1 < NT:
                        yield "PV", (k - LAG_PV, part)

        def events(k):
            a, b = k < A_STEPS, 0 <= k - LAG_B < A_STEPS
            turn = 0 <= k - LAG_OUT < A_STEPS and (k - LAG_OUT) % 4 == 3
            quartet = (k - LAG_OUT) // 4
            for half, at in enumerate((12, 19)):
                for g in next_groups(k, at):
                    yield "STACK", (g, half)
            if k in FIRST_AT:
                yield "FIRST", FIRST_AT.index(k) + 1
            for h in range(HG):
                for c in range(4):
                    stage = 4 * (k - PROJECT_FROM - 4 * c) + h
                    stages = PROJECT_STAGES if c < 3 else LAST_STAGES
                    if stage in stages:
                        yield stages[stage][0], (c, stages[stage][1])
                if a:
                    yield "A", (k, h)
                if a and h == 0:
                    yield from products_with_v(k, (0, 1, 2))
                if h == 0:
                    if turn:
                        yield "TURN", quartet
                    for at, c in QK_AT.items():
                        for g in next_groups(k, at + 1):
                            yield "PIECE1", (g, c)
                    if k > NT and k % NT == 1 and k <= A_STEPS + 1:
                        yield "KEY0", k // NT - 1
                if k < NT and h % 2:
                    yield "VALUES", (k // 2, 2 * (k % 2) + h // 2)
                if b:
                    yield "B", (k - LAG_B, h)
                if not a and h < 3:
                    yield from products_with_v(k, (h,))
                if h == (1 if a else 2) and 0 <= k - LAG_PV < A_STEPS and (k - LAG_PV) % 4 == 3:
                    yield "COPY_OUT", (k - LAG_PV) // 4
                if h == 1 and turn:
                    yield "OUT", quartet
                if h == 1 and k > NT and k % NT == 1 and k <= A_STEPS + 1:
                    yield "MAX", k // NT - 1
                if h >= 2:
                    for at, c in QK_AT.items():
                        for g in next_groups(k, at):
                            yield "QK", (g, c, h - 2)
            if b:
                yield "CUT", k - LAG_B
            if 0 <= k + 3 - LAG_OUT < A_STEPS and (k + 3 - LAG_OUT) % 4 == 3:
                yield "GLOB", (k + 3 - LAG_OUT) // 4
            for at, c in QK_AT.items():
                for g in next_groups(k, at + 1):
                    yield "SPLIT", (g, c)
            for at, (half, copies) in SLOTS_AT.items():
                for g in next_groups(k, at):
                    yield "SLOTS", (g, half, copies)

        def window(j):
            return (P if j == 0 else 0), (2 * P if j == NT - 1 else 3 * P)

        STACK_DMAS = 2 * HG

        MAX_STACKED = 16 * 3

        def stack_sem(g, half):
            return S[f"stack{g % 2}{half}"]

        def stacked(g):
            return 16 * STACK_DMAS * (g // 2 + 1)

        def attention_block(load, b):
            with nc.Block() as block:
                @block.sync
                def _(sp):
                    def stack(g, half):
                        q_cols = slice(half * HALF, (half + 1) * HALF)
                        k_cols = slice(WINDOW + half * HALF, WINDOW + (half + 1) * HALF)
                        sp.wait_ge(S["slots_ready"], 4 * (2 * g + half + 1))
                        sp.wait_ge(S["piece3_ready"], 2 * (2 * g + half + 1))
                        for h in range(HG):
                            sp.dma_start(q_stack[g % 2][0:KROWS, h, q_cols],
                                         piece[half][HD * h:HD * (h + 1), 0:TERMS, :]).then_inc(stack_sem(g, half), 16)
                            sp.dma_start(k_stack[g % 2][0:KROWS, h, k_cols],
                                         piece[half][HD * (HG + h):HD * (HG + h + 1), 1:SLOTS, :])\
                              .then_inc(stack_sem(g, half), 16)

                    for half in range(2):
                        stack(0, half)
                    for k in range(STEPS):
                        for kind, n in events(k):
                            if kind == "MAX":
                                sp.wait_ge(S["max_piece"], 3 * n + 3)
                                for i in range(3):
                                    sp.dma_start(q_stack[n % 2][KROWS + i:KROWS + i + 1, :, :], neg_max[i][:, :])\
                                      .then_inc(S["max_stacked"], 16)
                            elif kind == "TURN_ATTN" and n[1] == 0:
                                c = n[0]
                                if c == 0:
                                    sp.wait_ge(stack_sem(NG - 1, 1), stacked(NG - 1))
                                    load(sp, b, range(3))
                                    sp.wait_ge(S["first_row"], 1)
                                    load(sp, b, range(3, 4))
                            elif kind == "MOMENTS":
                                c = n[0]
                                sp.wait_ge(S["x2_ready"], 2 * c + 2)
                                sp.dma_start(out[bass.ds(b, 1), 512 * c:512 * (c + 1), :]
                                             .rearrange("o (t p) d -> p (o t) d", p=P),
                                             x_b[:, 4 * c:4 * c + 4, :]).then_inc(S["stored"], 16)
                            elif kind == "STACK":
                                g, half = n
                                if g >= 2:
                                    sp.wait_ge(S["b_full"], HG * (NT * (g - 2) + (NT if half else 9)))
                                stack(g, half)
                            elif kind == "NORMALISE":
                                c = n[0]
                                sp.wait_ge(S["stored"], 16 * (c + 1))
                                sp.wait_ge(S["xn_ready"], LATE_TILES + 4 * c + 4)
                                load(sp, (b + 1) % B, range(c, c + 1))
                    sp.wait_ge(S["stored"], 16 * 4)
                    for c in range(4):
                        sp.wait_ge(S[f"x_in{c}"], 2 * 16)

                @block.tensor
                def _(pe):
                    used = [0]

                    def misc_bank():
                        if used[0]:
                            pe.wait_ge(S["misc_free"], used[0])
                        used[0] += 1

                    def qk(g, c, k):
                        if k == 0:
                            misc_bank()
                        product = pe.matmul(misc[:, :], wqk_sb[:, g, k, :], xnT[:, k, 512 * c:512 * (c + 1)],
                                            start=(k == 0), stop=(k == KC - 1))
                        if k == KC - 1:
                            product.then_inc(S["misc_full"], 1)

                    def transpose_pair(u):
                        if u >= 2 * EARLY_NORMALISED:
                            pe.wait_ge(S["xn_ready"], 2 * u + 2 - 4 * EARLY_NORMALISED)
                        if u >= 2:
                            pe.wait_ge(S["xnT_ready"], u - 1)
                        for k in range(KC):
                            for i in range(2):
                                last = pe.transpose(bank[u % 2][:, k * 2 * P + i * P:k * 2 * P + (i + 1) * P],
                                                    xn[:, (2 * u + i) % 8, k * P:(k + 1) * P], ident)
                        last.then_inc(S["xnT_psum"], 1)

                    def turn_attn(c, pair):
                        u = 2 * c + pair
                        if u == 0:
                            pe.wait_ge(S["first_row"], 1)
                            pe.wait_ge(S["a_free"], NT * HG * NG)
                        if pair == 0:
                            pe.wait_ge(S["attn_ready"], 13 + c)
                        if 1 <= u < 7:
                            pe.wait_ge(S["proj_in_sbuf"], u)
                        if u == 7:
                            pe.wait_ge(S["exp_ready"], HG * A_STEPS)
                        for k in range(KC):
                            for i in range(2):
                                last = pe.transpose(attn_banks[u][:, k * 2 * P + i * P:k * 2 * P + (i + 1) * P],
                                                    attn[:, 2 * u + i, k * P:(k + 1) * P], ident)
                        last.then_inc(S["proj_in_psum"], 1)

                    def project(c, pair):
                        u = 2 * c + pair
                        pe.wait_ge(S["proj_in_sbuf"], u + 1)
                        if 1 <= u < 7:
                            pe.wait_ge(S["x2_ready"], u)
                        for i in range(2):
                            for k in range(KC):
                                last = pe.matmul(project_banks[u][:, i * D:(i + 1) * D],
                                                 attnT[:, u % 2, k, i * P:(i + 1) * P], wo_sb[:, k, :],
                                                 start=(k == 0), stop=(k == KC - 1))
                        last.then_inc(S["proj_psum"], 1)

                    def turn_xn(c, pair):
                        u = 2 * c + pair
                        pe.wait_ge(S["xn_ready"], LATE_TILES + 2 * u + 2)
                        if u >= 1:
                            pe.wait_ge(S["xnT_ready"], NT // 2 + u)
                        for k in range(KC):
                            for i in range(2):
                                last = pe.transpose(s_banks[:, 3, k * 2 * P + i * P:k * 2 * P + (i + 1) * P],
                                                    xn_late[:, (2 * u + i) % 8, k * P:(k + 1) * P], ident)
                        last.then_inc(S["xnT_psum"], 1)

                    def router_logits():
                        pe.wait_ge(S["xnT_ready"], NT)
                        for k in range(KC):
                            for g in range(4):
                                last = pe.matmul(s_banks[SP * g:SP * (g + 1), 2, :], gate_sb[:, k, :],
                                                 xnT[:, k, 512 * g:512 * (g + 1)],
                                                 start=(k == 0), stop=(k == KC - 1))
                        last.then_inc(S["gate_psum"], 1)
                        pe.wait_ge(S["gate_rows"], 1)
                        for c in range(4):
                            last = pe.transpose(bank[0][:, P * c:P * (c + 1)],
                                                strip_rows[:, P * c:P * (c + 1)], ident)
                        last.then_inc(S["gate_cols"], 1)

                    def values(u, part):
                        i, k = divmod(part, KC)
                        if u >= 2 and part == 0:
                            pe.wait_ge(S["v_ready"], u - 1)
                        product = pe.matmul(s_banks[:, u % 2, i * D:(i + 1) * D],
                                            xnT[:, k, (2 * u + i) * P:(2 * u + i + 1) * P], wv_sb[:, k, :],
                                            start=(k == 0), stop=(k == KC - 1))
                        if part == 3:
                            product.then_inc(S["v_psum"], 1)

                    def first_token(stage):
                        if stage == 0:
                            for g in range(NG):
                                for k in range(KC):
                                    last = pe.matmul(o_bank[:, g:g + 1], wqk_sb[:, g, k, :], xnT[:, k, 0:1],
                                                     start=(k == 0), stop=(k == KC - 1))
                        elif stage == 1:
                            pe.wait_ge(S["dve_step"], NG)
                            for k in range(KC):
                                for g in range(NG):
                                    last = pe.matmul(o_bank[:, 64 + k * SP:64 + (k + 1) * SP],
                                                     wback_sb[:, g, k * P:(k + 1) * P], first_scaled[:, g, :],
                                                     start=(g == 0), stop=(g == NG - 1))
                        elif stage == 2:
                            pe.wait_ge(S["dve_step"], NG + 1)
                            for k in range(KC):
                                for g in range(4):
                                    last = pe.matmul(s_banks[SP * g:SP * (g + 1), 2, :], uw[:, k, :],
                                                     xnT[:, k, 512 * g:512 * (g + 1)],
                                                     start=(k == 0), stop=(k == KC - 1))
                        elif stage == 3:
                            pe.wait_ge(S["act_step"], 1)
                            for c in range(4):
                                last = pe.transpose(o_bank[:, P * c:P * (c + 1)],
                                                    strip_rows[:, P * c:P * (c + 1)], ident)
                        elif stage == 4:
                            pe.wait_ge(S["dve_step"], NG + 2)
                            last = pe.transpose(s_banks[0:1, 2, 128:256], small[:, 0:1], ident)
                        elif stage == 5:
                            pe.wait_ge(S["dve_step"], NG + 4)
                            last = pe.matmul(s_banks[:, 2, 256:256 + H], ones[0:1, :], small[0:1, 32:32 + H],
                                             start=True, stop=True)
                        elif stage == 6:
                            pe.wait_ge(S["dve_step"], NG + 5)
                            pe.wait_ge(S["pool_step"], 1)
                            pe.wait_ge(S["v_ready"], 1)
                            last = pe.matmul(s_banks[:, 2, 0:H * VW], ones[0:1, :], v_sb[0:1, 0, 0:H * VW],
                                             start=True, stop=True)
                        elif stage == 7:
                            pe.wait_ge(S["act_step"], 2)
                            pe.wait_ge(S["v_ready"], NT // 2)
                            for m in range(NT):
                                s = m // 4
                                tile = 4 * (m % 4) + m // 4
                                last = pe.matmul(o_bank[SP * s:SP * (s + 1), 0:H * VW], pgT[:, m, :],
                                                 v_sb[:, tile, 0:H * VW], start=(m % 4 == 0), stop=(m % 4 == 3))
                        elif stage == 8:
                            pe.wait_ge(S["dve_step"], NG + 8)
                            last = pe.matmul(s_banks[0:1, 2, 0:H * VW], ones[:, 0:1], masked_o0,
                                             start=True, stop=True)
                        last.then_inc(S["pe_step"], 1)

                    def first_qk(c):
                        pe.wait_ge(S["xnT_ready"], 2 * c + 2)
                        for k in range(KC):
                            qk(0, c, k)

                    for u in range(0, 4):
                        transpose_pair(u)
                        if u % 2:
                            first_qk(u // 2)
                    first_token(0)
                    for u in range(4, 8):
                        transpose_pair(u)
                    first_qk(2)
                    first_qk(3)
                    for k in range(STEPS):
                        for kind, n in events(k):
                            if kind == "FIRST":
                                first_token(n)
                            elif kind == "VALUES":
                                values(*n)
                            elif kind == "TURN_ATTN":
                                turn_attn(*n)
                            elif kind == "PROJECT":
                                project(*n)
                            elif kind == "TURN_XN":
                                turn_xn(*n)
                            elif kind == "LOGITS":
                                router_logits()
                            elif kind == "A":
                                n, h = n
                                g, t = divmod(n, NT)
                                if h == 0 and (t == 0 or t == 7):
                                    pe.wait_ge(stack_sem(g, int(t == 7)), stacked(g))
                                i = HG * n + h
                                if i >= len(a_ring):
                                    pe.wait_ge(S["a_free"], i - len(a_ring) + 1)
                                for s in range(4):
                                    q = P * t + SP * s
                                    last = pe.matmul(a_ring[i % len(a_ring)][SP * s:SP * (s + 1), 0:WIN],
                                                     q_stack[g % 2][0:KROWS, h, q:q + SP],
                                                     k_stack[g % 2][0:KROWS, h, q:q + WIN],
                                                     start=True, stop=True)
                                last.then_inc(S["a_full"], 1)
                            elif kind == "QK":
                                qk(*n)
                            elif kind == "MAX":
                                pe.wait_ge(S["max_ready"], n + 1)
                                misc_bank()
                                pe.transpose(misc[0:NT * HG, 0:P],
                                             row_max[:, n, :, :].rearrange("p h t -> p (h t)"), ident)\
                                  .then_inc(S["misc_full"], 1)
                            elif kind == "B":
                                n, h = n
                                g, j = divmod(n, NT)
                                c0, c1 = window(j)
                                if j == 0 and h == 0:
                                    pe.wait_ge(S["max_stacked"], MAX_STACKED * (g + 1))
                                i = HG * n + h
                                if i >= S_RING:
                                    pe.wait_ge(S["exp_ready"], i - S_RING + 1)
                                pe.matmul(s_banks[:, i % S_RING, c0:c1],
                                          k_stack[g % 2][0:SROWS, h, WINDOW + P * j:WINDOW + P * (j + 1)],
                                          q_stack[g % 2][0:SROWS, h, P * (j - 1) + c0:P * (j - 1) + c1],
                                          start=True, stop=True).then_inc(S["b_full"], 1)
                            elif kind == "PV":
                                n, part = n
                                g, i = divmod(n, NT)
                                j = i - 1 + part
                                pe.wait_ge(S["band_ready"], band_count(NT * g + j))
                                first, final = part == 0 or i == 0 and part == 1, part == 2 or j == NT - 1
                                if first and n % 4 == 0 and n:
                                    pe.wait_ge(S["o_copied"], n // 4)
                                for h in range(HG):
                                    head = HG * g + h
                                    last = pe.matmul(
                                        o_bank[SP * h:SP * (h + 1), P * (i % 4):P * (i % 4 + 1)],
                                        v_sb[:, j, VW * head:VW * head + SP],
                                        probs[:, j % 4, h, P * (i - j + 1):P * (i - j + 2)],
                                        start=first, stop=final)
                                last.then_inc(S["pv_done"], 1)
                            elif kind == "TURN":
                                pe.wait_ge(S["o_copied"], n + 1)
                                misc_bank()
                                for i in range(4):
                                    last = pe.transpose(misc[:, P * i:P * (i + 1)], o_raw[:, P * i:P * (i + 1)],
                                                        ident)
                                last.then_inc(S["misc_full"], 1)

                @block.scalar
                def _(act):
                    used = [0]

                    turned = [0]

                    def piece1(g, c):
                        used[0] += 1
                        if g >= 1:
                            act.wait_ge(stack_sem(g - 1, c // 2), stacked(g - 1))
                        act.wait_ge(S["misc_full"], used[0])
                        act.activation(piece[c // 2][:, 0, 512 * (c % 2):512 * (c % 2 + 1)], misc[:, :], ACT.Copy)\
                           .then_inc(S["piece1_ready"], 1)

                    def take_xnT(u):
                        act.wait_ge(S["xnT_psum"], u + 1)
                        act.activation(xnT[:, :, 2 * P * u:2 * P * (u + 1)],
                                       bank[u % 2][:, :].rearrange("p (k n) -> p k n", k=KC),
                                       ACT.Copy).then_inc(S["xnT_ready"], 1)

                    for u in range(8):
                        take_xnT(u)
                        if u == 1 or u == 3:
                            piece1(0, u // 2)
                    act.wait_ge(S["xn_ready"], LATE_TILES)
                    piece1(0, 2)
                    piece1(0, 3)
                    for k in range(STEPS):
                        for kind, n in events(k):
                            if kind == "VALUES" and n[1] == 3:
                                n = n[0]
                                act.wait_ge(S["v_psum"], n + 1)
                                act.activation(v_heads[:, 2 * n:2 * n + 2, :, 0:HD],
                                               s_banks[:, n % 2, :].rearrange("p (t h c) -> p t h c", t=2, c=HD),
                                               ACT.Copy).then_inc(S["v_ready"], 1)
                            elif kind == "TURN_XN":
                                u = 2 * n[0] + n[1]
                                act.wait_ge(S["xnT_psum"], NT // 2 + u + 1)
                                act.activation(xnT[:, :, 2 * P * u:2 * P * (u + 1)],
                                               s_banks[:, 3, :].rearrange("p (k n) -> p k n", k=KC),
                                               ACT.Copy).then_inc(S["xnT_ready"], 1)
                            elif kind == "LOGITS":
                                act.wait_ge(S["gate_psum"], 1)
                                act.activation(strip_rows, s_banks[:, 2, :], ACT.Copy)\
                                   .then_inc(S["gate_rows"], 1)
                            elif kind == "FIRST" and n == 2:
                                act.wait_ge(S["pe_step"], 3)
                                act.activation(strip_rows, s_banks[:, 2, :], ACT.Copy)\
                                   .then_inc(S["act_step"], 1)
                            elif kind == "FIRST" and n == 5:
                                act.wait_ge(S["dve_step"], NG + 6)
                                act.activation(pgT[:, :, 0:H], sg_arg, ACT.Exp, scale=LOGIT_SCALE)\
                                   .then_inc(S["act_step"], 1)
                            elif kind == "PIECE1":
                                piece1(*n)
                            elif kind == "MAX":
                                used[0] += 1
                                act.wait_ge(S["p0_arg_ready"], n + 1)
                                act.activation(p0[:, n, :, :], p0_arg[:, :, :], ACT.Exp,
                                               scale=LOGIT_SCALE).then_inc(S["p0_ready"], 1)
                            elif kind == "B":
                                n, h = n
                                g, j = divmod(n, NT)
                                c0, c1 = window(j)
                                if n >= 4 and h == 0:
                                    act.wait_ge(S["pv_done"], pv_count(n - 3, 0))
                                i = HG * n + h
                                act.wait_ge(S["b_full"], i + 1)
                                act.activation(probs[:, j % 4, h, c0:c1], s_banks[:, i % S_RING, c0:c1],
                                               ACT.Exp, scale=LOGIT_SCALE).then_inc(S["exp_ready"], 1)
                            elif kind == "COPY_OUT":
                                act.wait_ge(S["pv_done"], pv_count(4 * n + 3, 2))
                                if n:
                                    act.wait_ge(S["misc_full"], turned[0])
                                act.activation(o_raw[:, :], o_bank[:, :], ACT.Copy).then_inc(S["o_copied"], 1)
                            elif kind == "TURN":
                                used[0] += 1
                                turned[0] = used[0]

                @block.gpsimd
                def _(pool):
                    def piece3(g, c):
                        n = 4 * g + c
                        if g >= 1:
                            pool.wait_ge(stack_sem(g - 1, c // 2), stacked(g - 1))
                        pool.wait_ge(S["piece2_ready"], n + 1)
                        cols = slice(512 * (c % 2), 512 * (c % 2 + 1))
                        pool.tensor_tensor(piece[c // 2][:, SLOT_PIECE3, cols], rest[:, c % 2, :],
                                           piece[c // 2][:, SLOT_PIECE2, cols], ALU.subtract)\
                            .then_inc(S["piece3_ready"], 1)

                    inverse_deviation(pool, 3, 0)
                    piece3(0, 0)
                    piece3(0, 1)
                    piece3(0, 2)
                    piece3(0, 3)
                    pool.memset(v_heads[:, :, :, HD], 1.0)
                    pool.memset(v_sb[:, :, H * VW:], 0.0)
                    pool.memset(pgT[:, :, H:SP], 0.0).then_inc(S["pool_step"], 1)
                    for k in range(STEPS):
                        for kind, n in events(k):
                            if kind == "SPLIT":
                                piece3(*n)
                            elif kind == "MOMENTS":
                                inverse_deviation(pool, n[0], LATE_CHUNKS + n[0])
                            elif kind == "NEXT":
                                for c in range(EARLY_CHUNKS):
                                    inverse_deviation(pool, c, LATE_CHUNKS + 4 + c)
                            elif kind == "CUT":
                                g, j = divmod(n, NT)
                                pool.wait_ge(S["exp_ready"], HG * (n + 1))
                                if j > 0:
                                    part = probs[:, j % 4, :, 0:P]
                                    pool.affine_select(out=part, in_=part, compare_op=ALU.is_ge, fill=0.0,
                                                       base=0, pattern=[[0, HG], [1, P]],
                                                       channel_multiplier=-1).then_inc(S["band_ready"], 1)
                                if j < NT - 1:
                                    part = probs[:, j % 4, :, 2 * P:3 * P]
                                    pool.affine_select(out=part, in_=part, compare_op=ALU.is_ge, fill=0.0,
                                                       base=0, pattern=[[0, HG], [-1, P]],
                                                       channel_multiplier=1).then_inc(S["band_ready"], 1)
                            elif kind == "GLOB":
                                g, quartet = divmod(n, 4)
                                pool.wait_ge(S["p0_ready"], g + 1)
                                if n:
                                    pool.wait_ge(S["o_added"], n)
                                pool.tensor_tensor(
                                    glob_term[:, :, :, :],
                                    v0_all[:, VW * HG * g:VW * HG * (g + 1)]
                                    .rearrange("p (o h c) -> p o h c", o=1, c=VW).to_broadcast([P, 4, HG, VW]),
                                    p0[:, g, 4 * quartet:4 * quartet + 4, :].unsqueeze(3)
                                    .to_broadcast([P, 4, HG, VW]), ALU.mult).then_inc(S["glob_ready"], 1)

                @block.vector
                def _(dve):
                    used = [0]

                    def split(g, c):
                        n = 4 * g + c
                        used[0] += 1
                        half = piece[c // 2]
                        cols = slice(512 * (c % 2), 512 * (c % 2 + 1))
                        dve.wait_ge(S["piece1_ready"], n + 1)
                        if n >= 2:
                            dve.wait_ge(S["piece3_ready"], n - 1)
                        dve.tensor_tensor(rest[:, c % 2, :], misc[:, :], half[:, 0, cols], ALU.subtract)\
                           .then_inc(S["misc_free"], 1)
                        if g >= 1:
                            dve.wait_ge(stack_sem(g - 1, c // 2), stacked(g - 1))
                        dve.wait_ge(S["misc_free"], used[0])
                        dve.tensor_copy(half[:, SLOT_PIECE2, cols], rest[:, c % 2, :]).then_inc(S["piece2_ready"], 1)

                    def fill_slots(g, half, copies):
                        n = 2 * g + half
                        dve.wait_ge(S["piece2_ready"], 2 * n + 2)
                        for i in copies:
                            to, frm = ((1, 0), (4, 0), (6, 0), (3, SLOT_PIECE2))[i]
                            dve.tensor_copy(piece[half][:, to, :], piece[half][:, frm, :])\
                               .then_inc(S["slots_ready"], 1)

                    def first_token(stage):
                        dve.wait_ge(S["pe_step"], stage + 1)
                        if stage == 0:
                            for g in range(NG):
                                dve.tensor_scalar(first_scaled[:, g, :], pick[:, g, :], o_bank[:, g:g + 1], None,
                                                  ALU.mult).then_inc(S["dve_step"], 1)
                        elif stage == 1:
                            dve.tensor_copy(uw[:, :, :], o_bank[:, 64:64 + KC * SP]
                                            .rearrange("p (k c) -> p k c", k=KC))\
                               .then_inc(S["dve_step"], 1)
                        elif stage == 2:
                            dve.wait_ge(S["act_step"], 1)
                            dve.tensor_reduce(small[:, 0:1], strip_rows, AX.X, ALU.max)\
                               .then_inc(S["dve_step"], 1)
                        elif stage == 3:
                            dve.tensor_copy(s0T[:, :, :].rearrange("p (g c) h -> p g c h", g=4),
                                            o_bank[:, :].rearrange("p (c g e) -> p g c e", c=4, g=4)
                                            [:, :, :, H:2 * H]).then_inc(S["dve_step"], 1)
                        elif stage == 4:
                            dve.tensor_reduce(small[0:1, 32:32 + SP],
                                              s_banks[0:1, 2, 128:256].rearrange("p (g e) -> p e g", g=4),
                                              AX.X, ALU.max).then_inc(S["dve_step"], 1)
                        elif stage == 5:
                            dve.tensor_copy(small[:, 8:8 + H], s_banks[:, 2, 256:256 + H])\
                               .then_inc(S["dve_step"], 1)
                            dve.wait_ge(S["dve_step"], NG + 5)
                            dve.tensor_tensor(sg_arg, o_bank[:, :].rearrange("p (m e) -> p m e", m=NT)[:, :, 0:H],
                                              small[:, 8:8 + H].unsqueeze(1).to_broadcast([P, NT, H]),
                                              ALU.subtract).then_inc(S["dve_step"], 1)
                        elif stage == 6:
                            dve.tensor_copy(v0_all[:, :], s_banks[:, 2, 0:H * VW])\
                               .then_inc(S["dve_step"], 1)
                        elif stage == 7:
                            dve.tensor_tensor(masked_o0, o_bank[:, 0:H * VW], diag, ALU.mult)\
                               .then_inc(S["dve_step"], 1)
                        elif stage == 8:
                            dve.tensor_copy(o0_row, s_banks[0:1, 2, 0:H * VW])\
                               .then_inc(S["dve_step"], 1)
                            dve.wait_ge(S["dve_step"], NG + 9)
                            heads = o0_row.rearrange("p (h c) -> p h c", c=VW)
                            dve.reciprocal(small[0:1, 48:48 + H], heads[:, :, HD])\
                               .then_inc(S["dve_step"], 1)
                            dve.wait_ge(S["dve_step"], NG + 10)
                            dve.tensor_tensor(o0_norm, heads[:, :, 0:HD],
                                              small[0:1, 48:48 + H].unsqueeze(2).to_broadcast([1, H, HD]),
                                              ALU.mult)

                    moments(dve, 3, 0)
                    dve.wait_ge(S["xnT_psum"], 2)
                    normalise(dve, 2, xn)
                    split(0, 0)
                    split(0, 1)
                    fill_slots(0, 0, range(4))
                    first_token(0)
                    dve.wait_ge(S["rstd_ready"], 1)
                    dve.wait_ge(S["xnT_psum"], 4)
                    normalise(dve, 3, xn)
                    split(0, 2)
                    split(0, 3)
                    fill_slots(0, 1, range(4))
                    for k in range(STEPS):
                        for kind, n in events(k):
                            if kind == "FIRST":
                                first_token(n)
                            elif kind == "TURN_ATTN":
                                u = 2 * n[0] + n[1]
                                if u == 0:
                                    dve.wait_ge(stack_sem(NG - 1, 0), stacked(NG - 1))
                                if u >= 2:
                                    dve.wait_ge(S["proj_psum"], u - 1)
                                dve.wait_ge(S["proj_in_psum"], u + 1)
                                dve.tensor_copy(attnT[:, u % 2, :, :],
                                                attn_banks[u].rearrange("p (k n) -> p k n", k=KC))\
                                   .then_inc(S["proj_in_sbuf"], 1)
                            elif kind == "PROJECT":
                                c, u = n[0], 2 * n[0] + n[1]
                                dve.wait_ge(S[f"x_in{c}"], 16)
                                dve.wait_ge(S["proj_psum"], u + 1)
                                dve.tensor_tensor(x_b[:, 2 * u:2 * u + 2, :],
                                                  project_banks[u].rearrange("p (t d) -> p t d", t=2),
                                                  x_b[:, 2 * u:2 * u + 2, :], ALU.add)\
                                   .then_inc(S["x2_ready"], 1)
                            elif kind == "MOMENTS":
                                dve.wait_ge(S["x2_ready"], 2 * n[0] + 2)
                                moments(dve, n[0], 4 * (LATE_CHUNKS + n[0]))
                            elif kind == "NORMALISE":
                                c = n[0]
                                dve.wait_ge(S["rstd_ready"], LATE_CHUNKS + c + 1)
                                if c >= 2:
                                    dve.wait_ge(S["xnT_psum"], NT // 2 + 2 * c - 2)
                                normalise(dve, c, xn_late)
                            elif kind == "NEXT":
                                early_moments(dve, 2, LATE_CHUNKS + 4)
                            elif kind == "LOGITS":
                                dve.wait_ge(S["gate_cols"], 1)
                                dve.tensor_copy(
                                    logits[:, bass.ds(b * NT, NT), :].rearrange("p (g c) e -> p g c e", g=4),
                                    bank[0][:, :].rearrange("p (c g e) -> p g c e", c=4, g=4)[:, :, :, 0:E])
                            elif kind == "KEY0":
                                dve.wait_ge(S["a_free"], NT * HG * (n + 1))
                                maxima = row_max[:, n, :, :].rearrange("p h t -> p t h")
                                dve.tensor_tensor(maxima, maxima, s0T[:, :, HG * n:HG * n + HG], ALU.max)\
                                   .then_inc(S["max_ready"], 1)
                            elif kind == "A":
                                n, h = n
                                g, t = divmod(n, NT)
                                mask = band[0 if t == 0 else 2 if t == NT - 1 else 1]
                                i = HG * n + h
                                dve.wait_ge(S["a_full"], i + 1)
                                dve.tensor_tensor_reduce(
                                    out=a_ring[i % len(a_ring)][:, 0:WIN], in0=a_ring[i % len(a_ring)][:, 0:WIN], in1=mask,
                                    scale=1.0, scalar=con[:, C_LOWEST:C_LOWEST + 1], op0=ALU.add,
                                    op1=ALU.max, accum_out=row_max[:, g, h, t:t + 1]).then_inc(S["a_free"], 1)
                            elif kind == "SPLIT":
                                split(*n)
                            elif kind == "SLOTS":
                                fill_slots(*n)
                            elif kind == "MAX":
                                used[0] += 1
                                if n:
                                    dve.wait_ge(S["max_stacked"], MAX_STACKED * n)
                                    dve.wait_ge(S["p0_ready"], n)
                                dve.wait_ge(S["misc_full"], used[0])
                                turned = misc[0:NT * HG, 0:P]
                                dve.tensor_scalar(neg_max[0][:, :], turned, -1.0, None, ALU.mult)\
                                   .then_inc(S["max_piece"], 1)
                                dve.wait_ge(S["max_ready"], n + 1)
                                dve.tensor_tensor(
                                    p0_arg[:, 1:NT, :], s0T[:, 1:NT, HG * n:HG * n + HG],
                                    row_max[:, n, :, 1:NT].rearrange("p h t -> p t h"), ALU.subtract)\
                                   .then_inc(S["p0_diff"], 1)
                                dve.memset(p0_arg[:, 0, :], MASKED)
                                dve.wait_ge(S["p0_diff"], n + 1)
                                dve.memset(p0_arg[0:1, 1, :], MASKED).then_inc(S["p0_arg_ready"], 1)
                                dve.wait_ge(S["max_piece"], 3 * n + 1)
                                dve.scalar_tensor_tensor(out=neg_rest[:, :], in0=turned, scalar=-1.0,
                                                         in1=neg_max[0][:, :], op0=ALU.mult, op1=ALU.subtract)\
                                   .then_inc(S["misc_free"], 1)
                                dve.wait_ge(S["misc_free"], used[0])
                                dve.tensor_copy(neg_max[1][:, :], neg_rest[:, :]).then_inc(S["max_piece"], 1)
                                dve.wait_ge(S["max_piece"], 3 * n + 2)
                                dve.tensor_tensor(neg_max[2][:, :], neg_rest[:, :], neg_max[1][:, :],
                                                  ALU.subtract).then_inc(S["max_piece"], 1)
                            elif kind == "OUT":
                                g, quartet = divmod(n, 4)
                                used[0] += 1
                                dve.wait_ge(S["misc_full"], used[0])
                                dve.wait_ge(S["glob_ready"], n + 1)
                                if n:
                                    dve.wait_ge(S["attn_ready"], n)
                                dve.tensor_tensor(
                                    o_add[:, :, :, :].rearrange("p t h c -> p (t h) c"),
                                    misc[:, :].rearrange("p (th c) -> p th c", c=SP)[:, :, 0:VW],
                                    glob_term[:, :, :, :].rearrange("p t h c -> p (t h) c"), ALU.add)\
                                   .then_inc(S["o_added"], 1)
                                dve.wait_ge(S["o_added"], n + 1)
                                dve.reciprocal(recip[:, :, :], o_add[:, :, :, HD]).then_inc(S["misc_free"], 1)
                                dve.wait_ge(S["misc_free"], used[0])
                                dve.tensor_tensor(
                                    attn[:, 4 * quartet:4 * quartet + 4, HG * HD * g:HG * HD * (g + 1)]
                                    .rearrange("p t (h c) -> p t h c", c=HD),
                                    o_add[:, :, :, 0:HD],
                                    recip[:, :, :].unsqueeze(3).to_broadcast([P, 4, HG, HD]), ALU.mult)\
                                   .then_inc(S["attn_ready"], 1)
                                if g == NG - 1 and quartet == 0:
                                    dve.wait_ge(S["attn_ready"], n + 1)
                                    dve.tensor_copy(attn[0:1, 0, :], o0_norm.rearrange("p h c -> p (h c)"))\
                                       .then_inc(S["first_row"], 1)
            reset()

        with nc.Fori(0, B // 2) as i:
            first_logits_block(i)
        first_any = route()
        with nc.If(first_any != 0):
            experts(x, x1)

        def load(sp, b, chunks):
            with sp.If(first_any != 0):
                load_batch(x1, b)(sp, chunks)
            with sp.Else():
                load_batch(x, b)(sp, chunks)

        with nc.Block() as block:
            @block.sync
            def _(sp):
                load(sp, 0, range(4))
                for c in range(4):
                    sp.wait_ge(S[f"x_in{c}"], 16)

            @block.vector
            def _(dve):
                early_moments(dve, 1, 0)

            @block.gpsimd
            def _(pool):
                for c in range(EARLY_CHUNKS):
                    inverse_deviation(pool, c, c)
        reset()
        with nc.Fori(0, B) as b:
            attention_block(load, b)
        second_any = route()
        with nc.If(second_any != 0):
            experts(out, out)


def constants():
    import numpy as np
    con = np.zeros((P, C_END), np.float32)
    con[:, C_IDENT:C_IDENT + P] = np.eye(P)
    r = np.arange(P)[:, None] % SP
    strip = np.arange(P)[:, None] // SP
    c = np.arange(WIN)[None, :]
    outside = (c < r) | (c > 2 * WINDOW + r)
    key_first = SP * strip - WINDOW + c
    key_last = P * (NT - 1) + key_first
    for i, bad in enumerate((outside | (key_first < 0), outside, outside | (key_last >= T))):
        con[:, C_BAND + i * WIN:C_BAND + (i + 1) * WIN] = np.where(bad, MASKED, 0.0)
    pick = con[:, C_PICK:C_PICK + NG * SP].reshape(P, NG, SP)
    pick = np.zeros((P, NG, SP), np.float32)
    for p in range(P):
        for g in range(NG):
            half, row = divmod(p, HG * HD)
            pick[p, g, H * half + HG * g + row // HD] = 1.0
    con[:, C_PICK:C_PICK + NG * SP] = pick.reshape(P, -1)
    diag = np.zeros((P, H, VW), np.float32)
    for p in range(P):
        if p % SP < H:
            diag[p, p % SP, :] = 1.0
    con[:, C_DIAG:C_DIAG + H * VW] = diag.reshape(P, -1)
    con[:, C_RANK:C_RANK + E] = E - np.arange(E)
    con[:, C_LOWEST] = MASKED
    return con


def chunked(w):
    return w.reshape(w.shape[0] // P, P, w.shape[1]).transpose(1, 0, 2)


def kernel(**inputs):
    import numpy as np
    import concourse.bacc as bacc
    from concourse.bass_utils import run_bass_kernel_spmd

    a = {k.replace("L0_", ""): np.asarray(v) for k, v in inputs.items()}
    wq, wk = a["attn_Wq"], a["attn_Wk"]
    n = HG * HD
    wqk = np.stack([np.concatenate([chunked(wq.T)[:, :, g * n:(g + 1) * n], chunked(wk.T)[:, :, g * n:(g + 1) * n]],
                                   axis=2) for g in range(NG)], axis=1)
    wback = np.stack([np.concatenate([wk[g * n:(g + 1) * n], wq[g * n:(g + 1) * n]], axis=0)
                      for g in range(NG)], axis=1)
    laid = {
        "x": a["attn_x"], "wqk": wqk, "wback": wback, "wv": chunked(a["attn_Wv"].T), "wo": chunked(a["attn_Wo"].T),
        "gate": chunked(a["ffn_gate_w"].T),
        "w1": np.stack([chunked(a["ffn_w1"][e].T) for e in range(E)]),
        "b1": a["ffn_b1"].reshape(E, KC, P).transpose(0, 2, 1),
        "w2": np.stack([chunked(a["ffn_w2"][e].T) for e in range(E)]),
        "b2": a["ffn_b2"], "consts": constants(),
    }
    nc = bacc.Bacc("TRN2", target_bir_lowering=False, num_devices=1)
    arrays, args = {}, {}
    for name, array in laid.items():
        arrays[f"in_{name}"] = np.ascontiguousarray(array)
        args[name] = nc.dram_tensor(f"in_{name}", array.shape, FP32, kind="ExternalInput").ap()
    x1 = nc.dram_tensor("x1_scratch", (B, T, D), FP32, kind="Internal").ap()
    out = nc.dram_tensor("out_x", (B, T, D), FP32, kind="ExternalOutput").ap()
    build(nc, x1=x1, out=out, **args)
    r = run_bass_kernel_spmd(nc, [arrays], core_ids=[0])
    return r.results[0]["out_x"]
```
